# Optimizing a Trainium2 kernel written in Bass

```python
import numpy as np
import jax
import jax.numpy as jnp

def _softmax(x, axis=-1):
    return jax.nn.softmax(x, axis=axis)

def _gelu(x):
    return jax.nn.gelu(x, approximate=True)

def _silu(x):
    return jax.nn.silu(x)

def _sigmoid(x):
    return jax.nn.sigmoid(x)

def _layernorm(x, axis=-1, eps=1e-05):
    m = jnp.mean(x, axis=axis, keepdims=True)
    v = jnp.var(x, axis=axis, keepdims=True)
    return (x - m) / jnp.sqrt(v + eps)

def _scatter_add(tgt, idx, src, axis=0):
    return tgt.at[idx].add(src)

def _segment_sum(src, seg, n):
    return jax.ops.segment_sum(src, seg, n)
kernel_name = 'mk_xattn_seq_d1_seqx_r4_87768b'

def setup_inputs(seed: int=0):
    np.random.seed(seed)
    _w = jnp.asarray

    def _rec_inputs():
        import jax
        import jax.numpy as jnp
        _rk = jax.random.key(seed)
        x = -0.0003929 + 0.9999 * jax.random.normal(jax.random.fold_in(_rk, 1), (8, 112, 512), jnp.float32)
        _lenS = 112 - jax.random.randint(jax.random.fold_in(_rk, 7), (8,), 0, max(1, 112 // 4) + 1, jnp.int32)
        _lenS2 = 375 - jax.random.randint(jax.random.fold_in(_rk, 8), (8,), 0, max(1, 375 // 4) + 1, jnp.int32)
        _ctx_2048P = jax.random.normal(jax.random.fold_in(_rk, 11), (8, 16, 512), jnp.float32)
        _ctx_2048c = jax.random.dirichlet(jax.random.fold_in(_rk, 511), 0.3 * jnp.ones((16,), jnp.float32), (8, 375))
        _ctx_2048t = jnp.einsum('bsk,bkd->bsd', _ctx_2048c, _ctx_2048P)
        _ctx_2048t = _ctx_2048t * jax.lax.rsqrt(jnp.mean(jnp.square(_ctx_2048t)) + 1e-12) * 0.953939
        ctx_2048 = -8.57375e-05 + 0.999917 * (_ctx_2048t + 0.3 * jax.random.normal(jax.random.fold_in(_rk, 611), (8, 375, 512), jnp.float32))
        _validS = jnp.arange(112)[None, :] < _lenS[:, None]
        _validS2 = jnp.arange(375)[None, :] < _lenS2[:, None]
        _causal = jnp.tril(jnp.ones((112, 112), dtype=bool))
        mask_BxS2_bf1 = jnp.ones((8, 375), dtype=bool)
        return (x, ctx_2048, mask_BxS2_bf1)
    x, ctx_2048, mask_BxS2_bf1 = _rec_inputs()

    def _L0_xattn_setup():
        import jax, jax.numpy as jnp
        import numpy as np
        HIDDEN = 512
        HEADS = 16
        HEAD_DIM = HIDDEN // HEADS
        LN_EPS = 1e-05
        GATE_INIT = 0.5

        def _layer_norm(x, gamma, beta):
            mu = jnp.mean(x, axis=-1, keepdims=True)
            var = jnp.mean(jnp.square(x - mu), axis=-1, keepdims=True)
            return (x - mu) * jax.lax.rsqrt(var + LN_EPS) * gamma + beta
        key = jax.random.key(seed)
        ks = jax.random.split(key, 8)
        B, T_TEXT, T_AUDIO = (4, 512, 375)
        s = 0.02
        return {'hidden_states': jax.random.normal(ks[0], (B, T_TEXT, HIDDEN), jnp.float32), 'audio_kv': jax.random.normal(ks[1], (B, T_AUDIO, HIDDEN), jnp.float32), 'audio_attention_mask': jnp.ones((B, T_AUDIO), dtype=bool), 'Wq': jax.random.normal(ks[2], (HIDDEN, HIDDEN), jnp.float32) * s, 'Wk': jax.random.normal(ks[3], (HIDDEN, HIDDEN), jnp.float32) * s, 'Wv': jax.random.normal(ks[4], (HIDDEN, HIDDEN), jnp.float32) * s, 'Wo': jax.random.normal(ks[5], (HIDDEN, HIDDEN), jnp.float32) * s, 'ln_gamma': jnp.ones((HIDDEN,), jnp.float32), 'ln_beta': jnp.zeros((HIDDEN,), jnp.float32), 'gate': jnp.array([GATE_INIT], jnp.float32)}
    _L0_xattn_all = _L0_xattn_setup()
    _L0_xattn_in = {k: v for k, v in _L0_xattn_all.items() if k in ('Wq', 'Wk', 'Wv', 'Wo', 'ln_gamma', 'ln_beta', 'gate')}
    del _L0_xattn_all
    return {'x': x, 'ctx_2048': ctx_2048, 'mask_BxS2_bf1': mask_BxS2_bf1, 'L0_xattn_Wq': _L0_xattn_in['Wq'], 'L0_xattn_Wk': _L0_xattn_in['Wk'], 'L0_xattn_Wv': _L0_xattn_in['Wv'], 'L0_xattn_Wo': _L0_xattn_in['Wo'], 'L0_xattn_ln_gamma': _L0_xattn_in['ln_gamma'], 'L0_xattn_ln_beta': _L0_xattn_in['ln_beta'], 'L0_xattn_gate': _L0_xattn_in['gate']}

def reference(x, ctx_2048, mask_BxS2_bf1, L0_xattn_Wq, L0_xattn_Wk, L0_xattn_Wv, L0_xattn_Wo, L0_xattn_ln_gamma, L0_xattn_ln_beta, L0_xattn_gate):
    import jax
    import jax.numpy as jnp

    def _L0_xattn_ref(hidden_states, audio_kv, audio_attention_mask, Wq, Wk, Wv, Wo, ln_gamma, ln_beta, gate):
        import jax, jax.numpy as jnp
        import numpy as np
        HIDDEN = 512
        HEADS = 16
        HEAD_DIM = HIDDEN // HEADS
        LN_EPS = 1e-05
        GATE_INIT = 0.5

        def _layer_norm(x, gamma, beta):
            mu = jnp.mean(x, axis=-1, keepdims=True)
            var = jnp.mean(jnp.square(x - mu), axis=-1, keepdims=True)
            return (x - mu) * jax.lax.rsqrt(var + LN_EPS) * gamma + beta
        B, Tt, D = hidden_states.shape
        Ta = audio_kv.shape[1]
        scale = HEAD_DIM ** (-0.5)
        a = _layer_norm(audio_kv, ln_gamma, ln_beta)
        Q = (hidden_states @ Wq.T).reshape(B, Tt, HEADS, HEAD_DIM).transpose(0, 2, 1, 3)
        K = (a @ Wk.T).reshape(B, Ta, HEADS, HEAD_DIM).transpose(0, 2, 1, 3)
        V = (a @ Wv.T).reshape(B, Ta, HEADS, HEAD_DIM).transpose(0, 2, 1, 3)
        scores = jnp.einsum('bhtd,bhsd->bhts', Q, K) * scale
        mask = audio_attention_mask[:, None, None, :]
        scores = jnp.where(mask, scores, jnp.float32(-jnp.inf))
        attn = jax.nn.softmax(scores, axis=-1)
        out = jnp.einsum('bhts,bhsd->bhtd', attn, V)
        out = out.transpose(0, 2, 1, 3).reshape(B, Tt, D)
        out = out @ Wo.T
        return hidden_states + jnp.tanh(gate) * out
    x = _L0_xattn_ref(x, ctx_2048, mask_BxS2_bf1, L0_xattn_Wq, L0_xattn_Wk, L0_xattn_Wv, L0_xattn_Wo, L0_xattn_ln_gamma, L0_xattn_ln_beta, L0_xattn_gate)
    return x

_drawn_inputs = setup_inputs


def setup_inputs(seed=0):
    import zlib

    import numpy as np

    out = dict(_drawn_inputs(seed))
    spreads = {'L0_xattn_ln_gamma': (1.0, 0.6), 'L0_xattn_ln_beta': (0.0, 0.8)}
    factors = {'L0_xattn_Wq': 8.0, 'L0_xattn_Wk': 8.0}
    for name, (base, spread) in spreads.items():
        noise = np.random.default_rng([zlib.crc32(name.encode()), seed]).standard_normal(out[name].shape)
        drawn = base * np.exp(spread * noise) if base else spread * noise
        out[name] = jnp.asarray(drawn.astype(out[name].dtype))
    for name, factor in factors.items():
        out[name] = (out[name] * factor).astype(out[name].dtype)
    return out
```

```python
from contextlib import ExitStack

import concourse.bass as bass
from concourse import mybir

F32 = mybir.dt.float32
F32R = mybir.dt.float32r
U8 = mybir.dt.uint8
ALU = mybir.AluOpType
ACT = mybir.ActivationFunctionType
AX = mybir.AxisListType

HEADS = 16
PER_QUAD = 4
EPS = 1e-5
MASKED = 2.0 ** 127 * 1.5
LEAST_MAX = -(2.0 ** 126)
DMA = 16


def build(nc, x, xT, ctx_in, mask4, wqT, wkT, wvT, woT, gamma, beta, gate, masks_dram, out):
    B, T, D = x.shape
    S = ctx_in.shape[1]
    C = 3
    P = S // C
    KB = D // 128
    HD = D // HEADS
    Q = HEADS // PER_QUAD
    SCALE = float(HD) ** -0.5
    PAIRS = (B - 2) // 2
    PACKED = 3 * HD + 1
    SE = S + S % 2
    assert P * C == S and Q == KB and PER_QUAD * HD == 128 and B % 2 == 0 and B >= 4

    with ExitStack() as stack:
        def sb(name, shape, dt=F32):
            return stack.enter_context(nc.sbuf_tensor(name, shape, dt))

        def sem(name):
            return stack.enter_context(nc.semaphore(name))

        ident = sb("ident", [128, 128])
        raw = sb("raw", [128, 2, KB, D])
        wk_hi, wk_lo = sb("wk_hi", [128, KB, D], F32R), sb("wk_lo", [128, KB, D], F32R)
        wv_hi, wv_lo = sb("wv_hi", [128, KB, D], F32R), sb("wv_lo", [128, KB, D], F32R)
        wq_hi, wq_lo = sb("wq_hi", [128, KB, D], F32R), sb("wq_lo", [128, KB, D], F32R)
        wo_hi, wo_lo = sb("wo_hi", [128, KB, D], F32R), sb("wo_lo", [128, KB, D], F32R)
        gam = sb("gam", [128, KB])
        bet = sb("bet", [128, KB])
        gate_sb = sb("gate_sb", [128, 1])
        gate_t = sb("gate_t", [128, 1])
        bias_k = sb("bias_k", [128, Q])
        bias_v = sb("bias_v", [128, Q])
        z = sb("z", [P, C, D])
        stats = sb("stats", [P, C, 6])
        mv = sb("mv", [P, C, 2])
        neg_mean = sb("neg_mean", [P, C])
        var_eps = sb("var_eps", [P, C])
        minus_half = sb("minus_half", [P, C])
        rstd = sb("rstd", [P, C])
        zt_hi, zt_lo = sb("zt_hi", [128, KB, SE], F32R), sb("zt_lo", [128, KB, SE], F32R)
        xt = sb("xt", [128, KB, 2 * T])
        xt_hi, xt_lo = sb("xt_hi", [128, KB, 2 * T], F32R), sb("xt_lo", [128, KB, 2 * T], F32R)
        q_hi, q_lo = sb("q_hi", [128, Q, 2 * T], F32R), sb("q_lo", [128, Q, 2 * T], F32R)
        k_hi, k_lo = sb("k_hi", [128, 2, S], F32R), sb("k_lo", [128, 2, S], F32R)
        kp = sb("kp", [128, HEADS, SE], F32R)
        qp = sb("qp", [128, HEADS, T], F32R)
        v = sb("v", [P, 2, C, D])
        probs = sb("probs", [128, 2, PER_QUAD, S])
        probs_t = sb("probs_t", [P, PER_QUAD, C, T])
        row_max = sb("row_max", [T, 2, PER_QUAD])
        nbias = sb("nbias", [T, 2, PER_QUAD])
        row_sum = sb("row_sum", [T, 2, PER_QUAD])
        row_inv = sb("row_inv", [T, 2, PER_QUAD])
        ot_hi, ot_lo = sb("ot_hi", [128, Q, T], F32R), sb("ot_lo", [128, Q, T], F32R)
        x_res = sb("x_res", [T, D])
        out_sb = sb("out_sb", [T, D])
        mask_u8 = sb("mask_u8", [B, PER_QUAD * S], U8)

        ps_s = stack.enter_context(nc.psum_tensor("ps_s", [128, PER_QUAD, 512], F32))
        ps_t = stack.enter_context(nc.psum_tensor("ps_t", [128, 2, 512], F32))
        ps = stack.enter_context(nc.psum_tensor("ps", [128, 2, 512], F32))

        ctx_loaded, xt_loaded, res_loaded = sem("ctx_loaded"), sem("xt_loaded"), sem("res_loaded")
        small_loaded, mask_loaded = sem("small_loaded"), sem("mask_loaded")
        raw_loaded = [sem(f"raw_loaded{i}") for i in range(2)]
        mask_stored = sem("mask_stored")
        k_packed = [sem(f"k_packed{q}") for q in range(Q)]
        q_packed = [sem(f"q_packed{q}") for q in range(Q)]
        out_stored = sem("out_stored")
        z_done, k_done, v_done, q_done = sem("z_done"), sem("k_done"), sem("v_done"), sem("q_done")
        bias_done, s_done, t_done = sem("bias_done"), sem("s_done"), sem("t_done")
        o_done, y_done = sem("o_done"), sem("y_done")
        zh_ready, kh_ready, qh_ready, oh_ready = sem("zh_ready"), sem("kh_ready"), sem("qh_ready"), sem("oh_ready")
        v_ready, exp_ready, pt_even, gate_ready = sem("v_ready"), sem("exp_ready"), sem("pt_even"), sem("gate_ready")
        wh_ready = sem("wh_ready")
        zl_ready, kl_ready, ql_ready, ol_ready = sem("zl_ready"), sem("kl_ready"), sem("ql_ready"), sem("ol_ready")
        y_ready, pt_odd, max_ready, nbias_ready = sem("y_ready"), sem("pt_odd"), sem("max_ready"), sem("nbias_ready")
        inv_ready, stats_ready, mv_ready, ln_stats = sem("inv_ready"), sem("stats_ready"), sem("mv_ready"), sem("ln_stats")
        bias_ready, wl_ready, mask_ready = sem("bias_ready"), sem("wl_ready"), sem("mask_ready")
        ident_zero, ident_ready, consts_ready = sem("ident_zero"), sem("ident_ready"), sem("consts_ready")
        var_ready, rstd_ready, z_ready = sem("var_ready"), sem("rstd_ready"), sem("z_ready")
        p_ready, xh_ready, xl_ready, wq_ready = sem("p_ready"), sem("xh_ready"), sem("xl_ready"), sem("wq_ready")

        def fixed(eng, value):
            return value if isinstance(value, int) else eng.to_reg(value)

        def odd_slot(j):
            return 2 * j + 1

        def even_slot(j):
            return 2 * j + 2

        block = stack.enter_context(nc.Block())

        @block.sync
        def _(sp):
            def load_ctx(b):
                sp.dma_start(z[:, :, :], ctx_in[b].rearrange("(p c) d -> p c d", c=C)).then_inc(ctx_loaded, DMA)

            def load_xt(p):
                sp.dma_start(xt[:, :, :], xT[p].rearrange("(k p) t -> p k t", p=128)).then_inc(xt_loaded, DMA)

            def load_weight(i, w):
                sp.dma_start(raw[:, i, :, :], w.rearrange("(k p) n -> p k n", p=128)).then_inc(raw_loaded[i], DMA)

            def pack_q(q, par):
                for rows, src in ((0, q_hi), (1, q_hi), (2, q_lo)):
                    sp.dma_start(qp[rows * HD:(rows + 1) * HD, PER_QUAD * q:PER_QUAD * (q + 1), :].bitcast(F32),
                                 src[:, q, par * T:(par + 1) * T].bitcast(F32)).then_inc(q_packed[q], DMA)

            def pack_k(q, b):
                for rows, src in ((0, k_hi), (1, k_lo), (2, k_hi)):
                    sp.dma_start(kp[rows * HD:(rows + 1) * HD, PER_QUAD * q:PER_QUAD * (q + 1), 0:S].bitcast(F32),
                                 src[:, q % 2, :].bitcast(F32)).then_inc(k_packed[q], DMA)
                sp.dma_start(kp[3 * HD:3 * HD + 1, PER_QUAD * q:PER_QUAD * (q + 1), 0:S].bitcast(F32),
                             masks_dram[b].rearrange("(o g s) -> o g s", o=1, g=PER_QUAD)).then_inc(k_packed[q], DMA)

            def slot(b, par_next, pair_next, first=False, xt_pair=None, has_next=True, load_next_ctx=True):
                for q in range(Q):
                    if has_next:
                        count = fixed(sp, 4 * b + q + 1)
                        sp.wait_ge(ctx_loaded, DMA)
                        sp.wait_ge(s_done, count)
                        count = fixed(sp, 4 * pair_next + q + 1)
                        sp.wait_ge(ctx_loaded, DMA)
                        sp.wait_ge(ql_ready, count)
                        pack_q(q, par_next)
                    for kq in {0: (), 1: (0,), 2: (1,), 3: (2, 3)}[q]:
                        if has_next:
                            count = fixed(sp, 4 * (b + 1) + kq + 1)
                            sp.wait_ge(ctx_loaded, DMA)
                            sp.wait_ge(kl_ready, count)
                            pack_k(kq, b + 1)
                    if q == 2:
                        if has_next and load_next_ctx:
                            count = fixed(sp, 4 * (b + 2))
                            sp.wait_ge(ctx_loaded, DMA)
                            sp.wait_ge(zl_ready, count)
                            load_ctx(b + 2)
                        if xt_pair is not None:
                            count = fixed(sp, xt_pair)
                            sp.wait_ge(ctx_loaded, DMA)
                            sp.wait_ge(xl_ready, count)
                            load_xt(xt_pair)
                        if not first:
                            count = fixed(sp, b)
                            sp.wait_ge(ctx_loaded, DMA)
                            sp.wait_ge(y_ready, count)
                            sp.dma_start(out[b - 1], out_sb[:, :]).then_inc(out_stored, DMA)
                    if q == 3:
                        if not first:
                            count = fixed(sp, DMA * b)
                            sp.wait_ge(ctx_loaded, DMA)
                            sp.wait_ge(out_stored, count)
                        sp.dma_start(x_res[:, :], x[b]).then_inc(res_loaded, DMA)

            load_ctx(0)
            for dst, src in ((gam, gamma), (bet, beta), (gate_sb, gate)):
                sp.dma_start(dst[:, :], src).then_inc(small_loaded, DMA)
            load_weight(0, wkT)
            sp.dma_start(mask_u8[:, :], mask4).then_inc(mask_loaded, DMA)
            load_xt(0)
            load_weight(1, wqT)
            sp.wait_ge(zl_ready, 4)
            load_ctx(1)
            sp.wait_ge(mask_ready, 1)
            sp.dma_start(masks_dram, probs[0:B, 0, :, :].rearrange("b g s -> b (g s)")).then_inc(mask_stored, DMA)
            sp.wait_ge(wl_ready, 1)
            sp.wait_ge(bias_done, 1)
            load_weight(0, wvT)
            sp.wait_ge(wq_ready, 2)
            load_weight(1, woT)
            sp.wait_ge(xl_ready, 1)
            load_xt(1)
            sp.wait_ge(mask_stored, DMA)
            for q in range(Q):
                sp.wait_ge(kl_ready, q + 1)
                pack_k(q, 0)
            for q in range(Q):
                sp.wait_ge(ql_ready, q + 1)
                pack_q(q, 0)

            slot(0, 1, 0, first=True)
            with sp.Fori(0, PAIRS - 1) as j:
                slot(odd_slot(j), 0, j + 1, xt_pair=j + 2)
                slot(even_slot(j), 1, j + 1)
            j = PAIRS - 1
            slot(odd_slot(j), 0, j + 1)
            slot(even_slot(j), 1, j + 1, load_next_ctx=False)
            slot(B - 1, 0, 0, has_next=False)
            sp.wait_ge(y_ready, B)
            sp.dma_start(out[B - 1], out_sb[:, :]).then_inc(out_stored, DMA)
            sp.wait_ge(out_stored, DMA * B)

        @block.tensor
        def _(pe):
            def part3(dst, lhs, rhs, first, last):
                nc.tensor.matmul(dst, lhs[0], rhs[0], start=first, stop=False)
                nc.tensor.matmul(dst, lhs[0], rhs[1], start=False, stop=False)
                return nc.tensor.matmul(dst, lhs[1], rhs[0], start=False, stop=last)

            def project_k(q, bank, ks):
                for k in ks:
                    cols = slice(128 * q, 128 * (q + 1))
                    mm = part3(ps[:, bank, 0:SE], (wk_hi[:, k, cols], wk_lo[:, k, cols]),
                               (zt_hi[:, k, :], zt_lo[:, k, :]), k == 0, k == KB - 1)
                if ks[-1] == KB - 1:
                    mm.then_inc(k_done, 1)

            def project_v(c, bank, ks):
                for k in ks:
                    keys = slice(P * c, P * (c + 1))
                    mm = part3(ps[0:P, bank, 0:D], (zt_hi[:, k, keys], zt_lo[:, k, keys]),
                               (wv_hi[:, k, :], wv_lo[:, k, :]), k == 0, k == KB - 1)
                if ks[-1] == KB - 1:
                    mm.then_inc(v_done, 1)

            def project_q(q, bank):
                for k in range(KB):
                    cols = slice(128 * q, 128 * (q + 1))
                    mm = part3(ps[:, bank, 0:2 * T], (wq_hi[:, k, cols], wq_lo[:, k, cols]),
                               (xt_hi[:, k, :], xt_lo[:, k, :]), k == 0, k == KB - 1)
                mm.then_inc(q_done, 1)

            def project_out(bank, ks):
                for k in ks:
                    mm = part3(ps[0:T, bank, 0:D], (ot_hi[:, k, :], ot_lo[:, k, :]),
                               (wo_hi[:, k, :], wo_lo[:, k, :]), k == 0, k == KB - 1)
                if ks[-1] == KB - 1:
                    mm.then_inc(y_done, 1)

            def transpose_z(k, bank):
                for c in range(C):
                    mm = nc.tensor.transpose(ps[:, bank, P * c:P * (c + 1)], z[:, c, 128 * k:128 * (k + 1)],
                                             ident[0:P, 0:P])
                mm.then_inc(z_done, 1)

            def sum_bias(which):
                for q in range(Q):
                    for k in range(KB):
                        mm = nc.tensor.matmul(ps[:, which, q:q + 1], raw[:, 0, k, 128 * q:128 * (q + 1)],
                                              bet[:, k:k + 1], start=(k == 0), stop=(k == KB - 1))
                mm.then_inc(bias_done, 1)

            def scores(b, q, first=False):
                pe.wait_ge(k_packed[q], 4 * DMA * (b + 1))
                pe.wait_ge(q_packed[q], 3 * DMA * (b + 1))
                for g in range(PER_QUAD):
                    if not first:
                        pe.wait_ge(exp_ready, 4 * (4 * b + q - 1) + g + 1)
                    h = PER_QUAD * q + g
                    mm = nc.tensor.matmul(ps_s[0:T, g, 0:SE], qp[0:PACKED, h, :], kp[0:PACKED, h, :],
                                          start=True, stop=True)
                mm.then_inc(s_done, 1)

            def transpose_p(n, par, g, first=False):
                pe.wait_ge(p_ready, 4 * n + g + 1)
                if not first or g >= 2:
                    pe.wait_ge(pt_odd if g % 2 else pt_even, 2 * n + g // 2)
                for c in range(C):
                    mm = nc.tensor.transpose(ps_t[0:P, g % 2, T * c:T * (c + 1)],
                                             probs[0:T, par, g, P * c:P * (c + 1)], ident[0:T, 0:T])
                mm.then_inc(t_done, 1)

            def times_v(b, q, par):
                n = 4 * b + q
                pe.wait_ge(pt_even, 2 * n + 2)
                pe.wait_ge(pt_odd, 2 * n + 2)
                pe.wait_ge(v_ready, 3 * b + 3)
                for c in range(C):
                    for g in range(PER_QUAD):
                        h = PER_QUAD * q + g
                        mm = nc.tensor.matmul(ps[HD * g:HD * (g + 1), 1, 0:T], v[:, par, c, HD * h:HD * (h + 1)],
                                              probs_t[:, g, c, :], start=(c == 0), stop=(c == C - 1))
                mm.then_inc(o_done, 1)

            def slot(b, par, first=False, last=False):
                scores(b, 0, first)
                if first:
                    pe.wait_ge(v_ready, 2)
                else:
                    pe.wait_ge(kl_ready, 4 * (b + 1))
                for g in range(PER_QUAD):
                    if not first:
                        transpose_p(4 * b - 1, 1, g)
                    project_v(2, 0, [g])
                if par == 1 and not last:
                    pe.wait_ge(xl_ready, xt_count(b))
                    pe.wait_ge(ol_ready, 4 * b - 1)
                    project_q(0, 1)
                    pe.wait_ge(v_ready, 3 * b + 3)
                    project_q(1, 0)
                    pe.wait_ge(ql_ready, q_count(b) + 1)
                    project_q(2, 1)
                    pe.wait_ge(ql_ready, q_count(b) + 2)
                    project_q(3, 0)
                    pe.wait_ge(ql_ready, q_count(b) + 3)
                    times_v(b - 1, 3, 1 - par)
                elif not first:
                    pe.wait_ge(ol_ready, 4 * b - 1)
                    times_v(b - 1, 3, 1 - par)
                scores(b, 1)
                transpose_p(4 * b, 0, 0, first)
                if not first:
                    pe.wait_ge(ol_ready, 4 * b)
                    if par == 1 and not last:
                        pe.wait_ge(ql_ready, q_count(b) + 4)
                    else:
                        pe.wait_ge(v_ready, 3 * b + 3)
                    project_out(0, [0, 1])
                transpose_p(4 * b, 0, 1, first)
                if not first:
                    project_out(0, [2, 3])
                transpose_p(4 * b, 0, 2, first)
                if not last:
                    pe.wait_ge(z_ready, b + 2)
                    transpose_z(0, 1)
                    if first:
                        pe.wait_ge(v_ready, 3)
                    else:
                        pe.wait_ge(y_ready, b)
                    transpose_z(1, 0)
                transpose_p(4 * b, 0, 3, first)
                if not last:
                    pe.wait_ge(zl_ready, 4 * (b + 1) + 1)
                    transpose_z(2, 1)
                    pe.wait_ge(zl_ready, 4 * (b + 1) + 2)
                    transpose_z(3, 0)
                    pe.wait_ge(zl_ready, 4 * (b + 1) + 3)
                times_v(b, 0, par)
                if not last:
                    pe.wait_ge(zl_ready, 4 * (b + 1) + 4)
                    project_k(0, 0, [0, 1, 2, 3])
                scores(b, 2)
                transpose_p(4 * b + 1, 1, 0)
                pe.wait_ge(ol_ready, 4 * b + 1)
                if not last:
                    project_k(1, 1, [0, 1])
                transpose_p(4 * b + 1, 1, 1)
                if not last:
                    project_k(1, 1, [2, 3])
                transpose_p(4 * b + 1, 1, 2)
                if not last:
                    pe.wait_ge(kl_ready, 4 * (b + 1) + 1)
                    project_v(0, 0, [0, 1])
                transpose_p(4 * b + 1, 1, 3)
                if not last:
                    project_v(0, 0, [2, 3])
                    pe.wait_ge(kl_ready, 4 * (b + 1) + 2)
                times_v(b, 1, par)
                scores(b, 3)
                transpose_p(4 * b + 2, 0, 0)
                if not last:
                    pe.wait_ge(v_ready, 3 * (b + 1) + 1)
                    project_k(2, 0, [0, 1, 2, 3])
                transpose_p(4 * b + 2, 0, 1)
                pe.wait_ge(ol_ready, 4 * b + 2)
                if not last:
                    project_v(1, 1, [0, 1])
                transpose_p(4 * b + 2, 0, 2)
                if not last:
                    project_v(1, 1, [2, 3])
                transpose_p(4 * b + 2, 0, 3)
                if not last:
                    pe.wait_ge(kl_ready, 4 * (b + 1) + 3)
                    project_k(3, 0, [0, 1, 2, 3])
                    pe.wait_ge(v_ready, 3 * (b + 1) + 2)
                times_v(b, 2, par)

            def q_count(b):
                return 2 * (b + 1)

            def xt_count(b):
                return (b + 1) // 2 + 1

            pe.wait_ge(ident_ready, 1)
            pe.wait_ge(consts_ready, 5)
            pe.wait_ge(z_ready, 1)
            transpose_z(0, 1)
            transpose_z(1, 0)
            pe.wait_ge(zl_ready, 1)
            transpose_z(2, 1)
            pe.wait_ge(zl_ready, 2)
            transpose_z(3, 0)
            pe.wait_ge(small_loaded, 3 * DMA)
            pe.wait_ge(raw_loaded[0], DMA)
            pe.wait_ge(zl_ready, 3)
            sum_bias(1)
            pe.wait_ge(zl_ready, 4)
            pe.wait_ge(wl_ready, 1)
            project_k(0, 0, [0, 1, 2, 3])
            pe.wait_ge(bias_ready, 1)
            project_k(1, 1, [0, 1, 2, 3])
            pe.wait_ge(kl_ready, 1)
            project_k(2, 0, [0, 1, 2, 3])
            pe.wait_ge(kl_ready, 2)
            project_k(3, 1, [0, 1, 2, 3])
            pe.wait_ge(wq_ready, 2)
            pe.wait_ge(xl_ready, 1)
            pe.wait_ge(kl_ready, 3)
            project_q(0, 0)
            pe.wait_ge(kl_ready, 4)
            project_q(1, 1)
            pe.wait_ge(ql_ready, 1)
            project_q(2, 0)
            pe.wait_ge(ql_ready, 2)
            project_q(3, 1)
            pe.wait_ge(raw_loaded[0], 2 * DMA)
            pe.wait_ge(ql_ready, 3)
            sum_bias(0)
            pe.wait_ge(wl_ready, 2)
            pe.wait_ge(ql_ready, 4)
            project_v(0, 1, [0, 1, 2, 3])
            pe.wait_ge(bias_ready, 2)
            project_v(1, 0, [0, 1, 2, 3])
            slot(0, 0, first=True)
            pe.wait_ge(wl_ready, 3)
            with pe.Fori(0, PAIRS) as j:
                xt_count = lambda b: j + 2
                slot(odd_slot(j), 1)
                slot(even_slot(j), 0)
            slot(B - 1, 1, last=True)
            n = 4 * B - 1
            for g in range(PER_QUAD):
                transpose_p(n, 1, g)
            pe.wait_ge(ol_ready, n)
            times_v(B - 1, 3, 1)
            pe.wait_ge(ol_ready, n + 1)
            pe.wait_ge(y_ready, B - 1)
            project_out(0, [0, 1, 2, 3])

        @block.scalar
        def _(act):
            def high(dst, src, done, count, ready, bias=0.0):
                act.wait_ge(done, count)
                nc.scalar.activation(dst, src, ACT.Identity, bias=bias).then_inc(ready, 1)

            def high_z(b, k, bank):
                high(zt_hi[:, k, 0:S], ps[:, bank, 0:S], z_done, 4 * b + k + 1, zh_ready)

            def high_k(b, q, bank, before):
                act.wait_ge(k_packed[before[1]], 4 * DMA * (before[0] + 1))
                high(k_hi[:, q % 2, :], ps[:, bank, 0:S], k_done, 4 * b + q + 1, kh_ready, bias_k[:, q:q + 1])

            def high_q(base, q, bank):
                high(q_hi[:, q, :], ps[:, bank, 0:2 * T], q_done, base + q + 1, qh_ready)

            def high_o(n, q):
                high(ot_hi[:, q, :], ps[:, 1, 0:T], o_done, n + 1, oh_ready, bias_v[:, q:q + 1])

            def copy_v(b, par, c, bank):
                act.wait_ge(v_done, 3 * b + c + 1)
                nc.scalar.activation(v[:, par, c, :], ps[0:P, bank, 0:D], ACT.Copy).then_inc(v_ready, 1)

            def exps(n, par, heads):
                for g in heads:
                    if g == 0:
                        act.wait_ge(nbias_ready, n + 1)
                    nc.scalar.activation(probs[0:T, par, g, :], ps_s[0:T, g, 0:S], ACT.Exp,
                                         bias=nbias[:, par, g:g + 1], scale=SCALE,
                                         accum_out=row_sum[:, par, g:g + 1]).then_inc(exp_ready, 1)

            def copy_pt(n, g):
                act.wait_ge(t_done, 4 * n + g + 1)
                nc.scalar.activation(probs_t[:, g, :, :].rearrange("p c t -> p (c t)"), ps_t[0:P, 0, 0:C * T],
                                     ACT.Copy).then_inc(pt_even, 1)

            def slot(b, par, first=False, last=False):
                n = 4 * b
                if not first:
                    copy_pt(n - 1, 0)
                exps(n, 0, [0, 1])
                if not first:
                    copy_pt(n - 1, 2)
                exps(n, 0, [2, 3])
                copy_v(b, par, 2, 0)
                if par == 1 and not last:
                    for q in range(Q):
                        act.wait_ge(q_packed[q], 3 * DMA * (b + 1))
                        high_q(2 * (b + 1), q, (1, 0, 1, 0)[q])
                if not first:
                    high_o(n - 1, 3)
                copy_pt(n, 0)
                exps(n + 1, 1, [0, 1])
                if not last:
                    exps(n + 1, 1, [2])
                copy_pt(n, 2)
                exps(n + 1, 1, [3] if not last else [2, 3])
                if not last:
                    for k in range(KB):
                        high_z(b + 1, k, (1, 0, 1, 0)[k])
                high_o(n, 0)
                if not last:
                    high_k(b + 1, 0, 0, (b, 2))
                copy_pt(n + 1, 0)
                exps(n + 2, 0, [0, 1])
                if not last:
                    high_k(b + 1, 1, 1, (b, 3))
                copy_pt(n + 1, 2)
                exps(n + 2, 0, [2, 3])
                if not last:
                    copy_v(b + 1, 1 - par, 0, 0)
                high_o(n + 1, 1)
                copy_pt(n + 2, 0)
                exps(n + 3, 1, [0])
                if not last:
                    high_k(b + 1, 2, 0, (b + 1, 0))
                exps(n + 3, 1, [1])
                if last:
                    copy_pt(n + 2, 2)
                exps(n + 3, 1, [2, 3])
                if not last:
                    copy_pt(n + 2, 2)
                    copy_v(b + 1, 1 - par, 1, 1)
                    high_k(b + 1, 3, 0, (b + 1, 1))
                high_o(n + 2, 2)

            act.wait_ge(small_loaded, 3 * DMA)
            nc.scalar.activation(gate_t[:, :], gate_sb[:, :], ACT.Tanh).then_inc(gate_ready, 1)
            act.wait_ge(gate_ready, 1)

            def split_high(w_hi, i, count, scale_of):
                act.wait_ge(raw_loaded[i], DMA * count)
                for k in range(KB):
                    nc.scalar.activation(w_hi[:, k, :], raw[:, i, k, :], ACT.Copy,
                                         scale=scale_of(k)).then_inc(wh_ready, 1)

            split_high(wk_hi, 0, 1, lambda k: gam[:, k:k + 1])
            for k in range(KB):
                high_z(0, k, (1, 0, 1, 0)[k])
            act.wait_ge(bias_ready, 1)
            for q in range(Q):
                if q < 2:
                    high(k_hi[:, q % 2, :], ps[:, q % 2, 0:S], k_done, q + 1, kh_ready, bias_k[:, q:q + 1])
                else:
                    high_k(0, q, q % 2, (0, q - 2))
            for q in range(Q):
                high_q(0, q, q % 2)
            split_high(wv_hi, 0, 2, lambda k: gam[:, k:k + 1])
            act.wait_ge(bias_ready, 2)
            copy_v(0, 0, 0, 1)
            copy_v(0, 0, 1, 0)
            split_high(wo_hi, 1, 2, lambda k: gate_t[:, 0:1])
            slot(0, 0, first=True)
            with act.Fori(0, PAIRS) as j:
                slot(odd_slot(j), 1)
                slot(even_slot(j), 0)
            slot(B - 1, 1, last=True)
            n = 4 * B - 1
            copy_pt(n, 0)
            copy_pt(n, 2)
            high_o(n, 3)

        @block.vector
        def _(dve):
            def low(dst, hi, src, high_ready, count, ready, bias=0.0):
                dve.wait_ge(high_ready, count)
                nc.vector.scalar_tensor_tensor(dst, src, bias, hi.bitcast(F32), ALU.add,
                                               ALU.subtract).then_inc(ready, 1)

            def low_z(b, k, bank):
                low(zt_lo[:, k, 0:S], zt_hi[:, k, 0:S], ps[:, bank, 0:S], zh_ready, 4 * b + k + 1, zl_ready)

            def low_k(b, q, bank):
                low(k_lo[:, q % 2, :], k_hi[:, q % 2, :], ps[:, bank, 0:S], kh_ready, 4 * b + q + 1, kl_ready,
                    bias_k[:, q:q + 1])

            def low_q(base, q, bank):
                low(q_lo[:, q, :], q_hi[:, q, :], ps[:, bank, 0:2 * T], qh_ready, base + q + 1, ql_ready)

            def low_o(n, q):
                low(ot_lo[:, q, :], ot_hi[:, q, :], ps[:, 1, 0:T], oh_ready, n + 1, ol_ready, bias_v[:, q:q + 1])

            def maxima(n, par):
                dve.wait_ge(s_done, n + 1)
                nc.vector.tensor_reduce(row_max[:, par, :], ps_s[0:T, :, 0:S], AX.X, ALU.max).then_inc(max_ready, 1)
                dve.wait_ge(max_ready, n + 1)
                nc.vector.tensor_scalar(nbias[:, par, :], row_max[:, par, :], LEAST_MAX, -SCALE, ALU.max,
                                        ALU.mult).then_inc(nbias_ready, 1)

            def inverses(n, par):
                dve.wait_ge(exp_ready, 4 * n + 4)
                nc.vector.reciprocal(row_inv[:, par, :], row_sum[:, par, :]).then_inc(inv_ready, 1)

            def copy_pt(n, g):
                dve.wait_ge(t_done, 4 * n + g + 1)
                nc.vector.tensor_copy(probs_t[:, g, :, :].rearrange("p c t -> p (c t)"),
                                      ps_t[0:P, 1, 0:C * T]).then_inc(pt_odd, 1)

            def ln_statistics(b):
                dve.wait_ge(ctx_loaded, DMA * (b + 1))
                for c in range(C):
                    nc.vector.bn_stats(stats[:, c, :], z[:, c, :]).then_inc(stats_ready, 1)
                count = fixed(dve, C * (b + 1))
                dve.wait_ge(ctx_loaded, DMA)
                dve.wait_ge(stats_ready, count)
                for c in range(C):
                    nc.vector.bn_aggr(mv[:, c, :], stats[:, c, :]).then_inc(mv_ready, 1)
                dve.wait_ge(mv_ready, C * (b + 1))
                nc.vector.tensor_scalar(neg_mean[:, :], mv[:, :, 0], -1.0, None, ALU.mult).then_inc(ln_stats, 1)
                nc.vector.tensor_scalar(var_eps[:, :], mv[:, :, 1], EPS, None, ALU.add).then_inc(ln_stats, 1)

            def residual(b):
                dve.wait_ge(y_done, b + 1)
                dve.wait_ge(res_loaded, DMA * (b + 1))
                nc.vector.tensor_tensor(out_sb[:, :], ps[0:T, 0, 0:D], x_res[:, :], ALU.add).then_inc(y_ready, 1)

            def slot(b, par, first=False, last=False):
                n = 4 * b
                maxima(n, 0)
                if not first:
                    copy_pt(n - 1, 1)
                if not last:
                    ln_statistics(b + 1)
                if not first:
                    copy_pt(n - 1, 3)
                inverses(n, 0)
                if par == 1 and not last:
                    for q in range(Q):
                        low_q(2 * (b + 1), q, (1, 0, 1, 0)[q])
                if not first:
                    low_o(n - 1, 3)
                maxima(n + 1, 1)
                copy_pt(n, 1)
                if not first:
                    residual(b - 1)
                if last:
                    copy_pt(n, 3)
                inverses(n + 1, 1)
                if not last:
                    low_z(b + 1, 0, 1)
                    low_z(b + 1, 1, 0)
                    copy_pt(n, 3)
                    low_z(b + 1, 2, 1)
                    low_z(b + 1, 3, 0)
                low_o(n, 0)
                if not last:
                    low_k(b + 1, 0, 0)
                maxima(n + 2, 0)
                copy_pt(n + 1, 1)
                if not last:
                    low_k(b + 1, 1, 1)
                if last:
                    copy_pt(n + 1, 3)
                inverses(n + 2, 0)
                if not last:
                    copy_pt(n + 1, 3)
                low_o(n + 1, 1)
                maxima(n + 3, 1)
                if not last:
                    low_k(b + 1, 2, 0)
                copy_pt(n + 2, 1)
                if last:
                    copy_pt(n + 2, 3)
                inverses(n + 3, 1)
                if not last:
                    copy_pt(n + 2, 3)
                    low_k(b + 1, 3, 0)
                low_o(n + 2, 2)

            def split_low(w_hi, w_lo, i, high_count, scale_of):
                for k in range(KB):
                    dve.wait_ge(wh_ready, high_count + k + 1)
                    lo = nc.vector.scalar_tensor_tensor(w_lo[:, k, :], raw[:, i, k, :], scale_of(k),
                                                        w_hi[:, k, :].bitcast(F32), ALU.mult, ALU.subtract)
                lo.then_inc(wl_ready, 1)

            def copy_bias(dst, bank, count):
                dve.wait_ge(bias_done, count)
                nc.vector.tensor_copy(dst[:, :], ps[:, bank, 0:Q]).then_inc(bias_ready, 1)

            ln_statistics(0)
            dve.wait_ge(mask_loaded, DMA)
            nc.vector.tensor_scalar(probs[0:B, 0, :, :].rearrange("b g s -> b (g s)"), mask_u8[:, :], -1.0, MASKED,
                                    ALU.add, ALU.mult).then_inc(mask_ready, 1)
            split_low(wk_hi, wk_lo, 0, 0, lambda k: gam[:, k:k + 1])
            for k in range(KB):
                low_z(0, k, (1, 0, 1, 0)[k])
            copy_bias(bias_k, 1, 1)
            dve.wait_ge(bias_ready, 1)
            for q in range(Q):
                low_k(0, q, q % 2)
            for q in range(Q):
                low_q(0, q, q % 2)
            copy_bias(bias_v, 0, 2)
            split_low(wv_hi, wv_lo, 0, KB, lambda k: gam[:, k:k + 1])
            dve.wait_ge(bias_ready, 2)
            split_low(wo_hi, wo_lo, 1, 2 * KB, lambda k: gate_t[:, 0:1])
            slot(0, 0, first=True)
            with dve.Fori(0, PAIRS) as j:
                slot(odd_slot(j), 1)
                slot(even_slot(j), 0)
            slot(B - 1, 1, last=True)
            n = 4 * B - 1
            copy_pt(n, 1)
            copy_pt(n, 3)
            low_o(n, 3)
            residual(B - 1)

        @block.gpsimd
        def _(pool):
            def normalise(b):
                pool.wait_ge(ln_stats, 2 * (b + 1))
                nc.gpsimd.tensor_tensor(rstd[:, :], var_eps[:, :], minus_half[:, :], ALU.pow).then_inc(rstd_ready, 1)
                count = fixed(pool, b + 1)
                pool.wait_ge(consts_ready, 5)
                pool.wait_ge(rstd_ready, count)
                for c in range(C):
                    last = nc.gpsimd.tensor_scalar(z[:, c, :], z[:, c, :], neg_mean[:, c:c + 1], rstd[:, c:c + 1],
                                                   ALU.add, ALU.mult)
                last.then_inc(z_ready, 1)

            def normalise_probs(n, par):
                count = fixed(pool, n + 1)
                pool.wait_ge(consts_ready, 5)
                pool.wait_ge(inv_ready, count)
                for g in range(PER_QUAD):
                    nc.gpsimd.tensor_scalar(probs[0:T, par, g, :], probs[0:T, par, g, :], row_inv[:, par, g:g + 1],
                                            1.0, ALU.mult, ALU.mult).then_inc(p_ready, 1)

            def split_xt(pair, first=False):
                pool.wait_ge(xt_loaded, DMA * (pair + 1))
                if not first:
                    count = fixed(pool, 4 * pair)
                    pool.wait_ge(consts_ready, 5)
                    pool.wait_ge(q_done, count)
                nc.gpsimd.tensor_copy(xt_hi[:, :, :], xt[:, :, :]).then_inc(xh_ready, 1)
                pool.wait_ge(xh_ready, pair + 1)
                nc.gpsimd.tensor_tensor(xt_lo[:, :, :], xt[:, :, :], xt_hi[:, :, :].bitcast(F32),
                                        ALU.subtract).then_inc(xl_ready, 1)

            def slot(b, par, pair=None, last=False):
                if pair is not None:
                    split_xt(pair)
                normalise_probs(4 * b, 0)
                if not last:
                    normalise(b + 1)
                for q in range(1, Q):
                    normalise_probs(4 * b + q, q % 2)

            nc.gpsimd.memset(minus_half[:, :], -0.5).then_inc(consts_ready, 1)
            pool.wait_ge(consts_ready, 1)
            nc.gpsimd.memset(qp[3 * HD:3 * HD + 1, :, :].bitcast(F32), 1.0).then_inc(consts_ready, 1)
            for i, padded in enumerate((zt_hi, zt_lo, kp)):
                pool.wait_ge(consts_ready, 2 + i)
                nc.gpsimd.memset(padded[:, :, S:SE].bitcast(F32), 0.0).then_inc(consts_ready, 1)
            pool.wait_ge(consts_ready, 5)
            nc.gpsimd.memset(ident[:, :], 0.0).then_inc(ident_zero, 1)
            pool.wait_ge(ident_zero, 1)
            nc.gpsimd.affine_select(out=ident[:, :], in_=ident[:, :], compare_op=ALU.not_equal, fill=1.0, base=0,
                                    pattern=[[-1, 128]], channel_multiplier=1).then_inc(ident_ready, 1)
            pool.wait_ge(consts_ready, 5)
            normalise(0)
            split_xt(0, first=True)
            pool.wait_ge(raw_loaded[1], DMA)
            nc.gpsimd.tensor_copy(wq_hi[:, :, :], raw[:, 1, :, :]).then_inc(wq_ready, 1)
            pool.wait_ge(wq_ready, 1)
            nc.gpsimd.tensor_tensor(wq_lo[:, :, :], raw[:, 1, :, :], wq_hi[:, :, :].bitcast(F32),
                                    ALU.subtract).then_inc(wq_ready, 1)
            slot(0, 0)
            with pool.Fori(0, PAIRS) as j:
                slot(odd_slot(j), 1, pair=j + 1)
                slot(even_slot(j), 0)
            slot(B - 1, 1, last=True)


def kernel(x, ctx_2048, mask_BxS2_bf1, L0_xattn_Wq, L0_xattn_Wk, L0_xattn_Wv, L0_xattn_Wo, L0_xattn_ln_gamma,
           L0_xattn_ln_beta, L0_xattn_gate):
    import numpy as np
    import concourse.bacc as bacc
    from concourse.bass_utils import run_bass_kernel_spmd

    B, T, D = x.shape
    S = ctx_2048.shape[1]
    C, HD, KB = 3, D // HEADS, D // 128

    def heads_inner(w):
        return w.T.reshape(D, D // 128, PER_QUAD, HD).transpose(0, 1, 3, 2).reshape(D, D)

    mask = np.asarray(mask_BxS2_bf1).view(np.uint8).reshape(B, 1, S // C, C).transpose(0, 1, 3, 2)
    arrays = {
        "x": x,
        "xT": np.asarray(x).reshape(B // 2, 2 * T, D).transpose(0, 2, 1),
        "ctx_in": ctx_2048,
        "mask4": np.broadcast_to(mask, (B, PER_QUAD, C, S // C)).reshape(B, PER_QUAD * S),
        "wqT": heads_inner(np.asarray(L0_xattn_Wq)),
        "wkT": heads_inner(np.asarray(L0_xattn_Wk)),
        "wvT": np.asarray(L0_xattn_Wv).T,
        "woT": np.asarray(L0_xattn_Wo).T,
        "gamma": np.asarray(L0_xattn_ln_gamma).reshape(KB, 128).T,
        "beta": np.asarray(L0_xattn_ln_beta).reshape(KB, 128).T,
        "gate": np.broadcast_to(np.asarray(L0_xattn_gate), (128, 1)),
    }
    arrays = {k: np.ascontiguousarray(a) for k, a in arrays.items()}
    nc = bacc.Bacc("TRN2", target_bir_lowering=False, num_devices=1)
    aps = {k: nc.dram_tensor(k, a.shape, mybir.dt.from_np(a.dtype), kind="ExternalInput").ap()
           for k, a in arrays.items()}
    masks_dram = nc.dram_tensor("masks_dram", (B, PER_QUAD * S), F32, kind="Internal").ap()
    out = nc.dram_tensor("out", (B, T, D), F32, kind="ExternalOutput").ap()
    build(nc, **aps, masks_dram=masks_dram, out=out)
    r = run_bass_kernel_spmd(nc, [arrays], core_ids=[0])
    return r.results[0]["out"]
```

```python
from contextlib import ExitStack

import concourse.bass as bass
from concourse import mybir

F32 = mybir.dt.float32
F32R = mybir.dt.float32r
U8 = mybir.dt.uint8
ALU = mybir.AluOpType
ACT = mybir.ActivationFunctionType
AX = mybir.AxisListType

HEADS = 16
PER_QUAD = 4
EPS = 1e-5
MASKED = 2.0 ** 127 * 1.5
LEAST_MAX = -(2.0 ** 126)
DMA = 16


def build(nc, x, xT, ctx_in, mask4, wqT, wkT, wvT, woT, gamma, beta, gate, masks_dram, out):
    B, T, D = x.shape
    S = ctx_in.shape[1]
    C = 3
    P = S // C
    KB = D // 128
    HD = D // HEADS
    Q = HEADS // PER_QUAD
    SCALE = float(HD) ** -0.5
    LOOPS = (B - 4) // 2
    PACKED = 3 * HD + 1
    SE = S + S % 2
    assert P * C == S and Q == KB and PER_QUAD * HD == 128 and B % 2 == 0 and B >= 6 and (C + 1) * T <= 512

    with ExitStack() as stack:
        def sb(name, shape, dt=F32):
            return stack.enter_context(nc.sbuf_tensor(name, shape, dt))

        def sem(name):
            return stack.enter_context(nc.semaphore(name))

        ident = sb("ident", [128, 128])
        raw = sb("raw", [128, 2, KB, D])
        wk_hi, wk_lo = sb("wk_hi", [128, KB, D], F32R), sb("wk_lo", [128, KB, D], F32R)
        wv_hi, wv_lo = sb("wv_hi", [128, KB, D], F32R), sb("wv_lo", [128, KB, D], F32R)
        wq_hi, wq_lo = sb("wq_hi", [128, KB, D], F32R), sb("wq_lo", [128, KB, D], F32R)
        wo_hi, wo_lo = sb("wo_hi", [128, KB, D], F32R), sb("wo_lo", [128, KB, D], F32R)
        gam = sb("gam", [128, KB])
        bet = sb("bet", [128, KB])
        gate_sb = sb("gate_sb", [128, 1])
        gate_t = sb("gate_t", [128, 1])
        bias_k = sb("bias_k", [128, Q])
        bias_v = sb("bias_v", [128, Q])
        z = sb("z", [P, C, D])
        stats = sb("stats", [P, C, 6])
        mv = sb("mv", [P, C, 2])
        neg_mean = sb("neg_mean", [P, C])
        var_eps = sb("var_eps", [P, C])
        minus_half = sb("minus_half", [P, C])
        rstd = sb("rstd", [P, C])
        zt_hi = sb("zt_hi", [128, 2, KB, SE], F32R)
        zt_lo = sb("zt_lo", [128, 2, KB, SE], F32R)
        xt = sb("xt", [128, KB, 2 * T])
        xt_hi, xt_lo = sb("xt_hi", [128, KB, 2 * T], F32R), sb("xt_lo", [128, KB, 2 * T], F32R)
        q_hi, q_lo = sb("q_hi", [128, Q, 2 * T], F32R), sb("q_lo", [128, Q, 2 * T], F32R)
        k_hi, k_lo = sb("k_hi", [128, 2, S], F32R), sb("k_lo", [128, 2, S], F32R)
        kp = sb("kp", [128, HEADS, SE], F32R)
        qp = sb("qp", [128, HEADS, T], F32R)
        v = sb("v", [P, 2, C, D])
        z_first = v[:, 1, :, :]
        probs = sb("probs", [128, 2, PER_QUAD, S])
        probs_t = sb("probs_t", [P, PER_QUAD, C, T])
        row_max = sb("row_max", [T, 2, PER_QUAD])
        nbias = sb("nbias", [T, 2, PER_QUAD])
        row_sum = sb("row_sum", [T, 2, PER_QUAD])
        row_inv = sb("row_inv", [T, 2, PER_QUAD])
        ot_hi = sb("ot_hi", [128, 2, Q, T], F32R)
        ot_lo = sb("ot_lo", [128, 2, Q, T], F32R)
        rows = sb("rows", [T, D])
        mask_u8 = rows[0:B, :].bitcast(U8)[:, 0:PER_QUAD * S]

        ps_s = stack.enter_context(nc.psum_tensor("ps_s", [128, PER_QUAD, 512], F32))
        ps_t = stack.enter_context(nc.psum_tensor("ps_t", [128, 2, 512], F32))
        ps = stack.enter_context(nc.psum_tensor("ps", [128, 2, 512], F32))
        ps_o = ps_t[:, 0, C * T:C * T + T]

        ctx_loaded, xt_loaded, x_loaded = sem("ctx_loaded"), sem("xt_loaded"), sem("x_loaded")
        ctx1_loaded = sem("ctx1_loaded")
        small_loaded, mask_loaded = sem("small_loaded"), sem("mask_loaded")
        raw_loaded = [sem(f"raw_loaded{i}") for i in range(2)]
        mask_stored = sem("mask_stored")
        k_packed = [sem(f"k_packed{q}") for q in range(Q)]
        q_packed = [sem(f"q_packed{q}") for q in range(Q)]
        out_stored = sem("out_stored")
        z_done, k_done, v_done, q_done = sem("z_done"), sem("k_done"), sem("v_done"), sem("q_done")
        bias_done, s_done, t_done = sem("bias_done"), sem("s_done"), sem("t_done")
        o_done, y_done = sem("o_done"), sem("y_done")
        zh_ready, kh_ready, qh_ready, oh_ready = sem("zh_ready"), sem("kh_ready"), sem("qh_ready"), sem("oh_ready")
        v_ready, exp_ready, pt_ready, gate_ready = sem("v_ready"), sem("exp_ready"), sem("pt_ready"), sem("gate_ready")
        wh_ready, xh0_ready = sem("wh_ready"), sem("xh0_ready")
        zl_ready, kl_ready, ql_ready, ol_ready = sem("zl_ready"), sem("kl_ready"), sem("ql_ready"), sem("ol_ready")
        y_ready, max_ready, nbias_ready = sem("y_ready"), sem("max_ready"), sem("nbias_ready")
        inv_ready, stats_ready, mv_ready, ln_stats = sem("inv_ready"), sem("stats_ready"), sem("mv_ready"), sem("ln_stats")
        bias_ready, wl_ready, mask_ready = sem("bias_ready"), sem("wl_ready"), sem("mask_ready")
        xl0_ready = sem("xl0_ready")
        ident_zero, ident_ready, consts_ready = sem("ident_zero"), sem("ident_ready"), sem("consts_ready")
        var_ready, rstd_ready, z_ready = sem("var_ready"), sem("rstd_ready"), sem("z_ready")
        p_ready, xh_ready, xl_ready = sem("p_ready"), sem("xh_ready"), sem("xl_ready")

        def fixed(eng, value):
            return value if isinstance(value, int) else eng.to_reg(value)

        def odd_slot(j):
            return 2 * j + 1

        def even_slot(j):
            return 2 * j + 2

        block = stack.enter_context(nc.Block())

        @block.sync
        def _(sp):
            def load_ctx(b):
                sp.dma_start(z[:, :, :], ctx_in[b].rearrange("(p c) d -> p c d", c=C)).then_inc(ctx_loaded, DMA)

            def load_xt(p):
                sp.dma_start(xt[:, :, :], xT[p].rearrange("(k p) t -> p k t", p=128)).then_inc(xt_loaded, DMA)

            def load_weight(i, w):
                sp.dma_start(raw[:, i, :, :], w.rearrange("(k p) n -> p k n", p=128)).then_inc(raw_loaded[i], DMA)

            def pack_q(q, par):
                for lines, src in ((0, q_hi), (1, q_hi), (2, q_lo)):
                    sp.dma_start(qp[lines * HD:(lines + 1) * HD, PER_QUAD * q:PER_QUAD * (q + 1), :].bitcast(F32),
                                 src[:, q, par * T:(par + 1) * T].bitcast(F32)).then_inc(q_packed[q], DMA)

            def pack_k(q, b):
                for lines, src in ((0, k_hi), (1, k_lo), (2, k_hi)):
                    sp.dma_start(kp[lines * HD:(lines + 1) * HD, PER_QUAD * q:PER_QUAD * (q + 1), 0:S].bitcast(F32),
                                 src[:, q % 2, :].bitcast(F32)).then_inc(k_packed[q], DMA)
                sp.dma_start(kp[3 * HD:3 * HD + 1, PER_QUAD * q:PER_QUAD * (q + 1), 0:S].bitcast(F32),
                             masks_dram[b].rearrange("(o g s) -> o g s", o=1, g=PER_QUAD)).then_inc(k_packed[q], DMA)

            def next_q(b, q, par_next, pair_next):
                count = fixed(sp, 4 * b + q + 1)
                sp.wait_ge(mask_stored, DMA)
                sp.wait_ge(s_done, count)
                count = fixed(sp, 4 * pair_next + q + 1)
                sp.wait_ge(mask_stored, DMA)
                sp.wait_ge(ql_ready, count)
                pack_q(q, par_next)

            def next_k(b, q):
                count = fixed(sp, 4 * (b - 1) + q + 1)
                sp.wait_ge(mask_stored, DMA)
                sp.wait_ge(s_done, count)
                count = fixed(sp, 4 * b + q + 1)
                sp.wait_ge(mask_stored, DMA)
                sp.wait_ge(kl_ready, count)
                pack_k(q, b)

            def slot(b, par_next, pair_next, first=False, last=False, xt_pair=None, load_ahead=True):
                if not first:
                    next_k(b, 3)
                else:
                    sp.wait_ge(kl_ready, 4)
                    pack_k(3, 0)
                if xt_pair is not None:
                    count = fixed(sp, xt_pair - 1)
                    sp.wait_ge(mask_stored, DMA)
                    sp.wait_ge(xl_ready, count)
                    load_xt(xt_pair)
                if not last:
                    next_q(b, 0, par_next, pair_next)
                if not first:
                    count = fixed(sp, b)
                    sp.wait_ge(mask_stored, DMA)
                    sp.wait_ge(y_ready, count)
                    sp.dma_start(out[b - 1], rows[:, :]).then_inc(out_stored, DMA)
                if not last:
                    next_q(b, 1, par_next, pair_next)
                    next_k(b + 1, 0)
                    next_q(b, 2, par_next, pair_next)
                if not first:
                    count = fixed(sp, DMA * b)
                    sp.wait_ge(mask_stored, DMA)
                    sp.wait_ge(out_stored, count)
                sp.dma_start(rows[:, :], x[b]).then_inc(x_loaded, DMA)
                if not last:
                    next_k(b + 1, 1)
                    next_q(b, 3, par_next, pair_next)
                    if load_ahead:
                        count = fixed(sp, 4 * (b + 3))
                        sp.wait_ge(mask_stored, DMA)
                        sp.wait_ge(z_done, count)
                        load_ctx(b + 3)
                    next_k(b + 1, 2)

            sp.dma_start(mask_u8, mask4).then_inc(mask_loaded, DMA)
            load_ctx(0)
            load_xt(0)
            for dst, src in ((gam, gamma), (bet, beta), (gate_sb, gate)):
                sp.dma_start(dst[:, :], src).then_inc(small_loaded, DMA)
            sp.dma_start(z_first, ctx_in[1].rearrange("(p c) d -> p c d", c=C)).then_inc(ctx1_loaded, DMA)
            sp.wait_ge(mask_ready, 1)
            sp.dma_start(masks_dram, probs[0:B, 0, :, :].rearrange("b g s -> b (g s)")).then_inc(mask_stored, DMA)
            sp.wait_ge(wl_ready, KB)
            load_weight(0, wvT)
            sp.wait_ge(xl0_ready, 1)
            load_xt(1)
            sp.wait_ge(wl_ready, 2 * KB)
            sp.wait_ge(bias_done, 1)
            load_weight(1, woT)
            sp.wait_ge(z_done, 4)
            load_ctx(2)
            sp.wait_ge(mask_stored, DMA)
            sp.wait_ge(ql_ready, 1)
            pack_q(0, 0)
            sp.wait_ge(kl_ready, 1)
            pack_k(0, 0)
            for q in range(1, Q):
                sp.wait_ge(ql_ready, q + 1)
                pack_q(q, 0)
                if q < 3:
                    sp.wait_ge(kl_ready, q + 1)
                    pack_k(q, 0)

            slot(0, 1, 0, first=True)
            with sp.Fori(0, LOOPS) as j:
                slot(odd_slot(j), 0, j + 1, xt_pair=j + 2)
                slot(even_slot(j), 1, j + 1)
            slot(B - 3, 0, LOOPS + 1, load_ahead=False)
            slot(B - 2, 1, LOOPS + 1, load_ahead=False)
            slot(B - 1, 0, 0, last=True)
            sp.wait_ge(y_ready, B)
            sp.dma_start(out[B - 1], rows[:, :]).then_inc(out_stored, DMA)
            sp.wait_ge(out_stored, DMA * B)

        @block.tensor
        def _(pe):
            def part3(dst, lhs, rhs, first, last):
                nc.tensor.matmul(dst, lhs[0], rhs[0], start=first, stop=False)
                nc.tensor.matmul(dst, lhs[0], rhs[1], start=False, stop=False)
                return nc.tensor.matmul(dst, lhs[1], rhs[0], start=False, stop=last)

            def project_k(q, par, bank, ks=range(KB)):
                for k in ks:
                    cols = slice(128 * q, 128 * (q + 1))
                    mm = part3(ps[:, bank, 0:SE], (wk_hi[:, k, cols], wk_lo[:, k, cols]),
                               (zt_hi[:, par, k, :], zt_lo[:, par, k, :]), k == 0, k == KB - 1)
                if ks[-1] == KB - 1:
                    mm.then_inc(k_done, 1)

            def project_v(c, par, bank, ks=range(KB)):
                for k in ks:
                    keys = slice(P * c, P * (c + 1))
                    mm = part3(ps[0:P, bank, 0:D], (zt_hi[:, par, k, keys], zt_lo[:, par, k, keys]),
                               (wv_hi[:, k, :], wv_lo[:, k, :]), k == 0, k == KB - 1)
                if ks[-1] == KB - 1:
                    mm.then_inc(v_done, 1)

            def project_q(q, bank, ks=range(KB)):
                for k in ks:
                    cols = slice(128 * q, 128 * (q + 1))
                    mm = part3(ps[:, bank, 0:2 * T], (wq_hi[:, k, cols], wq_lo[:, k, cols]),
                               (xt_hi[:, k, :], xt_lo[:, k, :]), k == 0, k == KB - 1)
                if ks[-1] == KB - 1:
                    mm.then_inc(q_done, 1)

            def project_out(par, bank, ks=range(KB)):
                for k in ks:
                    mm = part3(ps[0:T, bank, 0:D], (ot_hi[:, par, k, :], ot_lo[:, par, k, :]),
                               (wo_hi[:, k, :], wo_lo[:, k, :]), k == 0, k == KB - 1)
                if ks[-1] == KB - 1:
                    mm.then_inc(y_done, 1)

            def transpose_z(k, dst, src=z):
                for c in range(C):
                    mm = nc.tensor.transpose(dst[:, P * c:P * (c + 1)], src[:, c, 128 * k:128 * (k + 1)],
                                             ident[0:P, 0:P])
                mm.then_inc(z_done, 1)

            def sum_bias(i):
                for q in range(Q):
                    for k in range(KB):
                        mm = nc.tensor.matmul(ps_t[:, i, q:q + 1], raw[:, i, k, 128 * q:128 * (q + 1)],
                                              bet[:, k:k + 1], start=(k == 0), stop=(k == KB - 1))
                mm.then_inc(bias_done, 1)

            def scores(b, q, first=False):
                pe.wait_ge(k_packed[q], 4 * DMA * (b + 1))
                pe.wait_ge(q_packed[q], 3 * DMA * (b + 1))
                for g in range(PER_QUAD):
                    if not first:
                        pe.wait_ge(exp_ready, 4 * (4 * b + q - 1) + g + 1)
                    h = PER_QUAD * q + g
                    mm = nc.tensor.matmul(ps_s[0:T, g, 0:SE], qp[0:PACKED, h, :], kp[0:PACKED, h, :],
                                          start=True, stop=True)
                mm.then_inc(s_done, 1)

            def transpose_p(n, par, g):
                for c in range(C):
                    mm = nc.tensor.transpose(ps_t[0:P, g % 2, T * c:T * (c + 1)],
                                             probs[0:T, par, g, P * c:P * (c + 1)], ident[0:T, 0:T])
                mm.then_inc(t_done, 1)

            def transpose_first(n, par, first=False):
                pe.wait_ge(p_ready, 4 * n + 1)
                if not first:
                    pe.wait_ge(pt_ready, 4 * n - 1)
                    pe.wait_ge(ol_ready, n)
                transpose_p(n, par, 0)
                pe.wait_ge(p_ready, 4 * n + 2)
                if not first:
                    pe.wait_ge(pt_ready, 4 * n)
                transpose_p(n, par, 1)

            def transpose_second(n, par):
                pe.wait_ge(p_ready, 4 * n + 3)
                pe.wait_ge(pt_ready, 4 * n + 1)
                transpose_p(n, par, 2)
                pe.wait_ge(p_ready, 4 * n + 4)
                pe.wait_ge(pt_ready, 4 * n + 2)
                transpose_p(n, par, 3)

            def times_v(b, q, par):
                n = 4 * b + q
                pe.wait_ge(pt_ready, 4 * n + 4)
                for c in range(C):
                    for g in range(PER_QUAD):
                        h = PER_QUAD * q + g
                        mm = nc.tensor.matmul(ps_o[HD * g:HD * (g + 1), :], v[:, par, c, HD * h:HD * (h + 1)],
                                              probs_t[:, g, c, :], start=(c == 0), stop=(c == C - 1))
                mm.then_inc(o_done, 1)

            def slot(b, par, first=False, last=False, with_z=True):
                with_q = par == 1 and not last
                with_z = with_z and not last
                other = 0 if with_z else 1
                n = 4 * b
                scores(b, 0, first)
                if first:
                    pe.wait_ge(bias_ready, 2)
                else:
                    transpose_first(n - 1, 1)
                pe.wait_ge(kl_ready, 4 * b + 3)
                project_v(1, par, 0, [0])
                if not first:
                    transpose_second(n - 1, 1)
                project_v(1, par, 0, [1, 2, 3])
                if not first:
                    times_v(b - 1, 3, 1 - par)
                pe.wait_ge(v_ready, 3 * b + 1)
                project_v(2, par, 1, [0, 1])
                project_v(2, par, 1, [2, 3])
                pe.wait_ge(v_ready, 3 * b + 2)
                project_k(3, par, 0)
                scores(b, 1)
                transpose_first(n, 0, first)
                if with_z:
                    pe.wait_ge(z_ready, b + 3)
                    pe.wait_ge(v_ready, 3 * b + 3)
                    transpose_z(0, ps[:, 1, :])
                transpose_second(n, 0)
                if not first:
                    pe.wait_ge(ol_ready, n)
                    if with_z:
                        pe.wait_ge(kl_ready, 4 * b + 4)
                    else:
                        pe.wait_ge(v_ready, 3 * b + 3)
                    project_out(1 - par, other, [0, 1])
                pe.wait_ge(v_ready, 3 * b + 3)
                times_v(b, 0, par)
                if not first:
                    project_out(1 - par, other, [2, 3])
                if with_z:
                    pe.wait_ge(zl_ready, 4 * (b + 2) + 1)
                    transpose_z(1, ps[:, 1, :])
                if with_q:
                    pe.wait_ge(xl_ready, xt_count(b))
                    pe.wait_ge(y_ready, b)
                    project_q(0, 0)
                    pe.wait_ge(zl_ready, 4 * (b + 2) + 2)
                    project_q(1, 1)
                scores(b, 2)
                transpose_first(n + 1, 1)
                if not last:
                    if with_q:
                        pe.wait_ge(ql_ready, q_count(b) + 1)
                    elif with_z and not first:
                        pe.wait_ge(y_ready, b)
                    else:
                        pe.wait_ge(kl_ready, 4 * b + 4)
                    project_k(0, 1 - par, 0, [0])
                transpose_second(n + 1, 1)
                if not last:
                    project_k(0, 1 - par, 0, [1, 2, 3])
                times_v(b, 1, par)
                if with_q:
                    pe.wait_ge(ql_ready, q_count(b) + 2)
                    project_q(2, 1)
                elif with_z:
                    pe.wait_ge(zl_ready, 4 * (b + 2) + 2)
                    transpose_z(2, ps[:, 1, :])
                if not last:
                    if with_z:
                        pe.wait_ge(kl_ready, 4 * (b + 1) + 1)
                    else:
                        pe.wait_ge(y_ready, b)
                    project_k(1, 1 - par, other, [0])
                if not last:
                    project_k(1, 1 - par, other, [1, 2, 3])
                scores(b, 3)
                transpose_first(n + 2, 0)
                if with_q:
                    if with_z:
                        pe.wait_ge(ql_ready, q_count(b) + 3)
                        transpose_z(2, ps[:, 1, :])
                elif with_z:
                    pe.wait_ge(zl_ready, 4 * (b + 2) + 3)
                    transpose_z(3, ps[:, 1, :])
                transpose_second(n + 2, 0)
                if with_q:
                    pe.wait_ge(kl_ready, 4 * (b + 1) + 2)
                    project_q(3, 0)
                    times_v(b, 2, par)
                    if with_z:
                        pe.wait_ge(zl_ready, 4 * (b + 2) + 3)
                        transpose_z(3, ps[:, 1, :])
                    pe.wait_ge(ql_ready, q_count(b) + 4)
                    project_k(2, 1 - par, 0, [0])
                    project_k(2, 1 - par, 0, [1, 2, 3])
                    pe.wait_ge(zl_ready, 4 * (b + 2) + 4)
                    project_v(0, 1 - par, 1)
                elif not last:
                    if with_z:
                        pe.wait_ge(kl_ready, 4 * (b + 1) + 2)
                    else:
                        pe.wait_ge(kl_ready, 4 * (b + 1) + 1)
                    project_k(2, 1 - par, 0)
                    times_v(b, 2, par)
                    if with_z:
                        pe.wait_ge(zl_ready, 4 * (b + 2) + 4)
                    else:
                        pe.wait_ge(kl_ready, 4 * (b + 1) + 2)
                    project_v(0, 1 - par, 1, [0])
                    project_v(0, 1 - par, 1, [1, 2, 3])
                else:
                    times_v(b, 2, par)

            def q_count(b):
                return 2 * (b + 1)

            pe.wait_ge(xl0_ready, 1)
            for k in range(KB):
                pe.wait_ge(wl_ready, k + 1)
                project_q(0, 0, [k])
            pe.wait_ge(ident_ready, 1)
            pe.wait_ge(consts_ready, 4)
            pe.wait_ge(z_ready, 1)
            transpose_z(0, ps_s[:, 0, :])
            transpose_z(1, ps_s[:, 1, :])
            project_q(1, 1)
            transpose_z(2, ps_s[:, 2, :])
            transpose_z(3, ps_s[:, 3, :])
            pe.wait_ge(ql_ready, 1)
            project_q(2, 0)
            pe.wait_ge(small_loaded, 3 * DMA)
            pe.wait_ge(raw_loaded[1], DMA)
            sum_bias(1)
            pe.wait_ge(ql_ready, 2)
            project_q(3, 1)
            pe.wait_ge(ql_ready, 3)
            pe.wait_ge(zl_ready, 4)
            pe.wait_ge(wl_ready, 2 * KB)
            project_k(0, 0, 0)
            pe.wait_ge(ql_ready, 4)
            project_k(1, 0, 1)
            pe.wait_ge(z_ready, 2)
            transpose_z(0, ps_s[:, 0, :], z_first)
            transpose_z(1, ps_s[:, 1, :], z_first)
            pe.wait_ge(kl_ready, 1)
            project_k(2, 0, 0)
            transpose_z(2, ps_s[:, 2, :], z_first)
            transpose_z(3, ps_s[:, 3, :], z_first)
            pe.wait_ge(raw_loaded[0], 2 * DMA)
            sum_bias(0)
            pe.wait_ge(kl_ready, 2)
            pe.wait_ge(wl_ready, 3 * KB)
            project_v(0, 0, 1)
            pe.wait_ge(zl_ready, 8)
            slot(0, 0, first=True)
            pe.wait_ge(wl_ready, 4 * KB)
            with pe.Fori(0, LOOPS) as j:
                xt_count = lambda b: j + 1
                slot(odd_slot(j), 1)
                slot(even_slot(j), 0)
            xt_count = lambda b: (b - 1) // 2 + 1
            slot(B - 3, 1)
            slot(B - 2, 0, with_z=False)
            slot(B - 1, 1, last=True)
            n = 4 * B - 1
            transpose_first(n, 1)
            pe.wait_ge(kl_ready, 4 * B)
            project_out(1, 0, [0, 1])
            transpose_second(n, 1)
            project_out(1, 0, [2])
            times_v(B - 1, 3, 1)
            pe.wait_ge(ol_ready, n + 1)
            project_out(1, 0, [3])

        @block.scalar
        def _(act):
            def high(dst, src, done, count, ready, bias=0.0):
                act.wait_ge(done, count)
                nc.scalar.activation(dst, src, ACT.Identity, bias=bias).then_inc(ready, 1)

            def high_z(b, par, k, src):
                high(zt_hi[:, par, k, 0:S], src[:, 0:S], z_done, 4 * b + k + 1, zh_ready)

            def high_k(b, q, bank, before):
                if before is not None:
                    act.wait_ge(k_packed[before[1]], 4 * DMA * (before[0] + 1))
                high(k_hi[:, q % 2, :], ps[:, bank, 0:S], k_done, 4 * b + q + 1, kh_ready, bias_k[:, q:q + 1])

            def high_q(base, q, bank):
                high(q_hi[:, q, :], ps[:, bank, 0:2 * T], q_done, base + q + 1, qh_ready)

            def next_q(b, q, bank):
                act.wait_ge(q_packed[q], 3 * DMA * (b + 1))
                high_q(2 * (b + 1), q, bank)

            def high_o(n, par, q):
                high(ot_hi[:, par, q, :], ps_o, o_done, n + 1, oh_ready, bias_v[:, q:q + 1])

            def copy_v(b, par, c, bank):
                act.wait_ge(v_done, 3 * b + c + 1)
                nc.scalar.activation(v[:, par, c, :], ps[0:P, bank, 0:D], ACT.Copy).then_inc(v_ready, 1)

            def exps(n, par, heads):
                for g in heads:
                    if g == 0:
                        act.wait_ge(nbias_ready, n + 1)
                    nc.scalar.activation(probs[0:T, par, g, :], ps_s[0:T, g, 0:S], ACT.Exp,
                                         bias=nbias[:, par, g:g + 1], scale=SCALE,
                                         accum_out=row_sum[:, par, g:g + 1]).then_inc(exp_ready, 1)

            def copy_pt(n, heads):
                for g in heads:
                    act.wait_ge(t_done, 4 * n + g + 1)
                    nc.scalar.activation(probs_t[:, g, :, :].rearrange("p c t -> p (c t)"),
                                         ps_t[0:P, g % 2, 0:C * T], ACT.Copy).then_inc(pt_ready, 1)

            def slot(b, par, first=False, last=False, with_z=True):
                n = 4 * b
                with_q = par == 1 and not last
                with_z = with_z and not last
                if not first:
                    copy_v(b, par, 0, 1)
                    copy_pt(n - 1, [0, 1, 2, 3])
                exps(n, 0, [0, 1, 2])
                copy_v(b, par, 1, 0)
                exps(n, 0, [3])
                if not first:
                    high_o(n - 1, 1 - par, 3)
                copy_v(b, par, 2, 1)
                high_k(b, 3, 0, (b, 1))
                copy_pt(n, [0, 1])
                if with_z:
                    high_z(b + 2, par, 0, ps[:, 1, :])
                copy_pt(n, [2, 3])
                exps(n + 1, 1, [0, 1, 2, 3])
                if with_z:
                    high_z(b + 2, par, 1, ps[:, 1, :])
                high_o(n, par, 0)
                if with_q:
                    next_q(b, 0, 0)
                    next_q(b, 1, 1)
                copy_pt(n + 1, [0, 1, 2, 3])
                exps(n + 2, 0, [0])
                if not last:
                    high_k(b + 1, 0, 0, (b, 2))
                exps(n + 2, 0, [1, 2])
                if with_z and not with_q:
                    high_z(b + 2, par, 2, ps[:, 1, :])
                exps(n + 2, 0, [3])
                if with_q:
                    next_q(b, 2, 1)
                high_o(n + 1, par, 1)
                if not last:
                    high_k(b + 1, 1, 0 if with_z else 1, (b, 3))
                copy_pt(n + 2, [0, 1])
                if with_z:
                    high_z(b + 2, par, 2 if with_q else 3, ps[:, 1, :])
                copy_pt(n + 2, [2, 3])
                exps(n + 3, 1, [0])
                if with_q:
                    next_q(b, 3, 0)
                    exps(n + 3, 1, [1, 2])
                    high_z(b + 2, par, 3, ps[:, 1, :])
                    exps(n + 3, 1, [3])
                    high_o(n + 2, par, 2)
                    high_k(b + 1, 2, 0, (b + 1, 0))
                else:
                    exps(n + 3, 1, [1])
                    if not last:
                        high_k(b + 1, 2, 0, (b + 1, 0))
                    exps(n + 3, 1, [2, 3])
                    high_o(n + 2, par, 2)

            act.dma_start(raw[:, 0, :, :], wqT.rearrange("(k p) n -> p k n", p=128)).then_inc(raw_loaded[0], DMA)
            act.dma_start(raw[:, 1, :, :], wkT.rearrange("(k p) n -> p k n", p=128)).then_inc(raw_loaded[1], DMA)
            act.wait_ge(xt_loaded, DMA)
            nc.scalar.activation(xt_hi[:, :, :], xt[:, :, :], ACT.Copy).then_inc(xh0_ready, 1)

            def split_high(w_hi, i, scale_of):
                for k in range(KB):
                    nc.scalar.activation(w_hi[:, k, :], raw[:, i, k, :], ACT.Copy,
                                         scale=scale_of(k)).then_inc(wh_ready, 1)

            act.wait_ge(raw_loaded[0], DMA)
            split_high(wq_hi, 0, lambda k: 1.0)
            for k in range(KB):
                high_z(0, 0, k, ps_s[:, k, :])
                if k % 2:
                    high_q(0, k // 2, k // 2)
            act.wait_ge(small_loaded, 3 * DMA)
            act.wait_ge(raw_loaded[1], DMA)
            split_high(wk_hi, 1, lambda k: gam[:, k:k + 1])
            high_q(0, 2, 0)
            high_q(0, 3, 1)
            nc.scalar.activation(gate_t[:, :], gate_sb[:, :], ACT.Tanh).then_inc(gate_ready, 1)
            act.wait_ge(bias_ready, 1)
            high_k(0, 0, 0, None)
            high_k(0, 1, 1, None)
            for k in range(2):
                high_z(1, 1, k, ps_s[:, k, :])
            act.wait_ge(raw_loaded[0], 2 * DMA)
            split_high(wv_hi, 0, lambda k: gam[:, k:k + 1])
            high_k(0, 2, 0, (0, 0))
            for k in range(2, KB):
                high_z(1, 1, k, ps_s[:, k, :])
            act.wait_ge(gate_ready, 1)
            act.wait_ge(raw_loaded[1], 2 * DMA)
            split_high(wo_hi, 1, lambda k: gate_t[:, 0:1])
            copy_v(0, 0, 0, 1)
            slot(0, 0, first=True)
            with act.Fori(0, LOOPS) as j:
                slot(odd_slot(j), 1)
                slot(even_slot(j), 0)
            slot(B - 3, 1)
            slot(B - 2, 0, with_z=False)
            slot(B - 1, 1, last=True)
            n = 4 * B - 1
            copy_pt(n, [0, 1, 2, 3])
            high_o(n, 1, 3)

        @block.vector
        def _(dve):
            def low(dst, hi, src, high_ready, count, ready, bias=0.0):
                dve.wait_ge(high_ready, count)
                nc.vector.scalar_tensor_tensor(dst, src, bias, hi.bitcast(F32), ALU.add,
                                               ALU.subtract).then_inc(ready, 1)

            def low_z(b, par, k, src):
                low(zt_lo[:, par, k, 0:S], zt_hi[:, par, k, 0:S], src[:, 0:S], zh_ready, 4 * b + k + 1, zl_ready)

            def low_k(b, q, bank):
                low(k_lo[:, q % 2, :], k_hi[:, q % 2, :], ps[:, bank, 0:S], kh_ready, 4 * b + q + 1, kl_ready,
                    bias_k[:, q:q + 1])

            def low_q(base, q, bank):
                low(q_lo[:, q, :], q_hi[:, q, :], ps[:, bank, 0:2 * T], qh_ready, base + q + 1, ql_ready)

            def low_o(n, par, q):
                low(ot_lo[:, par, q, :], ot_hi[:, par, q, :], ps_o, oh_ready, n + 1, ol_ready, bias_v[:, q:q + 1])

            def maxima(n, par):
                dve.wait_ge(s_done, n + 1)
                nc.vector.tensor_reduce(row_max[:, par, :], ps_s[0:T, :, 0:S], AX.X, ALU.max).then_inc(max_ready, 1)
                dve.wait_ge(max_ready, n + 1)
                nc.vector.tensor_scalar(nbias[:, par, :], row_max[:, par, :], LEAST_MAX, -SCALE, ALU.max,
                                        ALU.mult).then_inc(nbias_ready, 1)

            def inverses(n, par):
                dve.wait_ge(exp_ready, 4 * n + 4)
                nc.vector.reciprocal(row_inv[:, par, :], row_sum[:, par, :]).then_inc(inv_ready, 1)

            def ln_statistics(b, src=z):
                for c in range(C):
                    nc.vector.bn_stats(stats[:, c, :], src[:, c, :]).then_inc(stats_ready, 1)
                count = fixed(dve, C * (b + 1))
                dve.wait_ge(ctx_loaded, DMA)
                dve.wait_ge(stats_ready, count)
                for c in range(C):
                    nc.vector.bn_aggr(mv[:, c, :], stats[:, c, :]).then_inc(mv_ready, 1)
                dve.wait_ge(mv_ready, C * (b + 1))
                nc.vector.tensor_scalar(neg_mean[:, :], mv[:, :, 0], -1.0, None, ALU.mult).then_inc(ln_stats, 1)
                nc.vector.tensor_scalar(var_eps[:, :], mv[:, :, 1], EPS, None, ALU.add).then_inc(ln_stats, 1)

            def residual(b, bank):
                dve.wait_ge(y_done, b + 1)
                dve.wait_ge(x_loaded, DMA * (b + 1))
                nc.vector.tensor_tensor(rows[:, :], ps[0:T, bank, 0:D], rows[:, :], ALU.add).then_inc(y_ready, 1)

            def slot(b, par, first=False, last=False, with_z=True):
                n = 4 * b
                with_q = par == 1 and not last
                with_z = with_z and not last
                base = 2 * (b + 1)
                maxima(n, 0)
                if with_z:
                    if first:
                        dve.wait_ge(z_ready, 2)
                    dve.wait_ge(ctx_loaded, DMA * (b + 2))
                    ln_statistics(b + 2)
                inverses(n, 0)
                if not first:
                    low_o(n - 1, 1 - par, 3)
                low_k(b, 3, 0)
                maxima(n + 1, 1)
                if with_z:
                    low_z(b + 2, par, 0, ps[:, 1, :])
                inverses(n + 1, 1)
                if not first:
                    residual(b - 1, 0 if with_z else 1)
                if with_z:
                    low_z(b + 2, par, 1, ps[:, 1, :])
                low_o(n, par, 0)
                if with_q:
                    low_q(base, 0, 0)
                    low_q(base, 1, 1)
                maxima(n + 2, 0)
                if not last:
                    low_k(b + 1, 0, 0)
                inverses(n + 2, 0)
                if with_q:
                    low_q(base, 2, 1)
                elif with_z:
                    low_z(b + 2, par, 2, ps[:, 1, :])
                low_o(n + 1, par, 1)
                if not last:
                    low_k(b + 1, 1, 0 if with_z else 1)
                maxima(n + 3, 1)
                if with_q:
                    low_z(b + 2, par, 2, ps[:, 1, :])
                    low_q(base, 3, 0)
                elif with_z:
                    low_z(b + 2, par, 3, ps[:, 1, :])
                if not with_q and not last:
                    low_k(b + 1, 2, 0)
                if with_q:
                    low_z(b + 2, par, 3, ps[:, 1, :])
                inverses(n + 3, 1)
                low_o(n + 2, par, 2)
                if with_q:
                    low_k(b + 1, 2, 0)

            def split_low(w_hi, w_lo, i, high_count, scale_of):
                for k in range(KB):
                    dve.wait_ge(wh_ready, high_count + k + 1)
                    nc.vector.scalar_tensor_tensor(w_lo[:, k, :], raw[:, i, k, :], scale_of(k),
                                                   w_hi[:, k, :].bitcast(F32), ALU.mult,
                                                   ALU.subtract).then_inc(wl_ready, 1)

            def copy_bias(dst, i, count):
                dve.wait_ge(bias_done, count)
                nc.vector.tensor_copy(dst[:, :], ps_t[:, i, 0:Q]).then_inc(bias_ready, 1)

            dve.wait_ge(mask_loaded, DMA)
            nc.vector.tensor_scalar(probs[0:B, 0, :, :].rearrange("b g s -> b (g s)"), mask_u8, -1.0, MASKED,
                                    ALU.add, ALU.mult).then_inc(mask_ready, 1)
            dve.wait_ge(ctx_loaded, DMA)
            ln_statistics(0)
            dve.wait_ge(xh0_ready, 1)
            nc.vector.tensor_tensor(xt_lo[:, :, :], xt[:, :, :], xt_hi[:, :, :].bitcast(F32),
                                    ALU.subtract).then_inc(xl0_ready, 1)
            split_low(wq_hi, wq_lo, 0, 0, lambda k: 1.0)
            for k in range(KB):
                low_z(0, 0, k, ps_s[:, k, :])
                if k % 2:
                    low_q(0, k // 2, k // 2)
            dve.wait_ge(small_loaded, 3 * DMA)
            split_low(wk_hi, wk_lo, 1, KB, lambda k: gam[:, k:k + 1])
            copy_bias(bias_k, 1, 1)
            low_q(0, 2, 0)
            low_q(0, 3, 1)
            dve.wait_ge(z_ready, 1)
            dve.wait_ge(ctx1_loaded, DMA)
            ln_statistics(1, z_first)
            dve.wait_ge(bias_ready, 1)
            low_k(0, 0, 0)
            low_k(0, 1, 1)
            for k in range(2):
                low_z(1, 1, k, ps_s[:, k, :])
            split_low(wv_hi, wv_lo, 0, 2 * KB, lambda k: gam[:, k:k + 1])
            low_k(0, 2, 0)
            for k in range(2, KB):
                low_z(1, 1, k, ps_s[:, k, :])
            copy_bias(bias_v, 0, 2)
            dve.wait_ge(gate_ready, 1)
            split_low(wo_hi, wo_lo, 1, 3 * KB, lambda k: gate_t[:, 0:1])
            dve.wait_ge(bias_ready, 2)
            slot(0, 0, first=True)
            with dve.Fori(0, LOOPS) as j:
                slot(odd_slot(j), 1)
                slot(even_slot(j), 0)
            slot(B - 3, 1)
            slot(B - 2, 0, with_z=False)
            slot(B - 1, 1, last=True)
            n = 4 * B - 1
            low_o(n, 1, 3)
            residual(B - 1, 0)

        @block.gpsimd
        def _(pool):
            def normalise(b, src=z):
                pool.wait_ge(ln_stats, 2 * (b + 1))
                nc.gpsimd.tensor_tensor(rstd[:, :], var_eps[:, :], minus_half[:, :], ALU.pow).then_inc(rstd_ready, 1)
                count = fixed(pool, b + 1)
                pool.wait_ge(consts_ready, 4)
                pool.wait_ge(rstd_ready, count)
                for c in range(C):
                    last = nc.gpsimd.tensor_scalar(src[:, c, :], src[:, c, :], neg_mean[:, c:c + 1], rstd[:, c:c + 1],
                                                   ALU.add, ALU.mult)
                last.then_inc(z_ready, 1)

            def split_xt(pair):
                pool.wait_ge(xt_loaded, DMA * (pair + 1))
                count = fixed(pool, 4 * pair)
                pool.wait_ge(consts_ready, 4)
                pool.wait_ge(q_done, count)
                nc.gpsimd.tensor_copy(xt_hi[:, :, :], xt[:, :, :]).then_inc(xh_ready, 1)
                pool.wait_ge(xh_ready, pair)
                nc.gpsimd.tensor_tensor(xt_lo[:, :, :], xt[:, :, :], xt_hi[:, :, :].bitcast(F32),
                                        ALU.subtract).then_inc(xl_ready, 1)

            def normalise_probs(n, par):
                count = fixed(pool, n + 1)
                pool.wait_ge(consts_ready, 4)
                pool.wait_ge(inv_ready, count)
                for g in range(PER_QUAD):
                    nc.gpsimd.tensor_scalar(probs[0:T, par, g, :], probs[0:T, par, g, :], row_inv[:, par, g:g + 1],
                                            1.0, ALU.mult, ALU.mult).then_inc(p_ready, 1)

            def slot(b, xt_pair=None, with_z=True):
                if xt_pair is not None:
                    split_xt(xt_pair)
                if with_z:
                    normalise(b + 2)
                for q in range(Q):
                    normalise_probs(4 * b + q, q % 2)

            nc.gpsimd.memset(minus_half[:, :], -0.5).then_inc(consts_ready, 1)
            pool.wait_ge(consts_ready, 1)
            nc.gpsimd.memset(qp[3 * HD:3 * HD + 1, :, :].bitcast(F32), 1.0).then_inc(consts_ready, 1)
            pool.wait_ge(consts_ready, 2)
            nc.gpsimd.memset(ident[:, :], 0.0).then_inc(ident_zero, 1)
            pool.wait_ge(ident_zero, 1)
            nc.gpsimd.affine_select(out=ident[:, :], in_=ident[:, :], compare_op=ALU.not_equal, fill=1.0, base=0,
                                    pattern=[[-1, 128]], channel_multiplier=1).then_inc(ident_ready, 1)
            nc.gpsimd.memset(zt_hi[:, :, :, S:SE].bitcast(F32), 0.0)
            nc.gpsimd.memset(zt_lo[:, :, :, S:SE].bitcast(F32), 0.0).then_inc(consts_ready, 1)
            nc.gpsimd.memset(kp[:, :, S:SE].bitcast(F32), 0.0).then_inc(consts_ready, 1)
            pool.wait_ge(ident_ready, 1)
            pool.wait_ge(consts_ready, 4)
            normalise(0)
            normalise(1, z_first)
            slot(0)
            with pool.Fori(0, LOOPS) as j:
                slot(odd_slot(j), j + 1)
                slot(even_slot(j))
            slot(B - 3, LOOPS + 1)
            slot(B - 2, with_z=False)
            slot(B - 1, with_z=False)


def kernel(x, ctx_2048, mask_BxS2_bf1, L0_xattn_Wq, L0_xattn_Wk, L0_xattn_Wv, L0_xattn_Wo, L0_xattn_ln_gamma,
           L0_xattn_ln_beta, L0_xattn_gate):
    import numpy as np
    import concourse.bacc as bacc
    from concourse.bass_utils import run_bass_kernel_spmd

    B, T, D = x.shape
    S = ctx_2048.shape[1]
    C, HD, KB = 3, D // HEADS, D // 128

    def heads_inner(w):
        return w.T.reshape(D, D // 128, PER_QUAD, HD).transpose(0, 1, 3, 2).reshape(D, D)

    mask = np.asarray(mask_BxS2_bf1).view(np.uint8).reshape(B, 1, S // C, C).transpose(0, 1, 3, 2)
    arrays = {
        "x": x,
        "xT": np.asarray(x).reshape(B // 2, 2 * T, D).transpose(0, 2, 1),
        "ctx_in": ctx_2048,
        "mask4": np.broadcast_to(mask, (B, PER_QUAD, C, S // C)).reshape(B, PER_QUAD * S),
        "wqT": heads_inner(np.asarray(L0_xattn_Wq)),
        "wkT": heads_inner(np.asarray(L0_xattn_Wk)),
        "wvT": np.asarray(L0_xattn_Wv).T,
        "woT": np.asarray(L0_xattn_Wo).T,
        "gamma": np.asarray(L0_xattn_ln_gamma).reshape(KB, 128).T,
        "beta": np.asarray(L0_xattn_ln_beta).reshape(KB, 128).T,
        "gate": np.broadcast_to(np.asarray(L0_xattn_gate), (128, 1)),
    }
    arrays = {k: np.ascontiguousarray(a) for k, a in arrays.items()}
    nc = bacc.Bacc("TRN2", target_bir_lowering=False, num_devices=1)
    aps = {k: nc.dram_tensor(k, a.shape, mybir.dt.from_np(a.dtype), kind="ExternalInput").ap()
           for k, a in arrays.items()}
    masks_dram = nc.dram_tensor("masks_dram", (B, PER_QUAD * S), F32, kind="Internal").ap()
    out = nc.dram_tensor("out", (B, T, D), F32, kind="ExternalOutput").ap()
    build(nc, **aps, masks_dram=masks_dram, out=out)
    r = run_bass_kernel_spmd(nc, [arrays], core_ids=[0])
    return r.results[0]["out"]
```

```python
from contextlib import ExitStack

import concourse.bass as bass
from concourse import mybir

F32 = mybir.dt.float32
F32R = mybir.dt.float32r
U8 = mybir.dt.uint8
ALU = mybir.AluOpType
ACT = mybir.ActivationFunctionType
AX = mybir.AxisListType

HEADS = 16
PER_QUAD = 4
EPS = 1e-5
MASKED = 2.0 ** 127 * 1.5
LEAST_MAX = -(2.0 ** 126)
WARM_UP = 28
DMA = 16


def build(nc, x, xT, ctx_in, mask4, wqT, wkT, wvT, woT, gamma, beta, gate, masks_dram, out):
    B, T, D = x.shape
    S = ctx_in.shape[1]
    C = 3
    P = S // C
    KB = D // 128
    HD = D // HEADS
    Q = HEADS // PER_QUAD
    SCALE = float(HD) ** -0.5
    LOOPS = (B - 4) // 2
    PACKED = 3 * HD + 1
    POOL_WK, POOL_WV = 3, 2
    SE = S + S % 2
    assert P * C == S and Q == KB and PER_QUAD * HD == 128 and B % 2 == 0 and B >= 6 and (C + 1) * T <= 512

    with ExitStack() as stack:
        def sb(name, shape, dt=F32):
            return stack.enter_context(nc.sbuf_tensor(name, shape, dt))

        def sem(name):
            return stack.enter_context(nc.semaphore(name))

        ident = sb("ident", [128, 128])
        raw = sb("raw", [128, 2, KB, D])
        wk_hi, wk_lo = sb("wk_hi", [128, KB, D], F32R), sb("wk_lo", [128, KB, D], F32R)
        wv_hi, wv_lo = sb("wv_hi", [128, KB, D], F32R), sb("wv_lo", [128, KB, D], F32R)
        wq_hi, wq_lo = sb("wq_hi", [128, KB, D], F32R), sb("wq_lo", [128, KB, D], F32R)
        wo_hi, wo_lo = sb("wo_hi", [128, KB, D], F32R), sb("wo_lo", [128, KB, D], F32R)
        gam = sb("gam", [128, KB])
        bet = sb("bet", [128, KB])
        gate_sb = sb("gate_sb", [128, 1])
        gate_t = sb("gate_t", [128, 1])
        z = sb("z", [P, C, D])
        stats = sb("stats", [P, C, 6])
        mv = sb("mv", [P, C, 2])
        neg_mean = sb("neg_mean", [P, C])
        var_eps = sb("var_eps", [P, C])
        minus_half = sb("minus_half", [P, C])
        rstd = sb("rstd", [P, C])
        zt_full = sb("zt_full", [128, 2, S])
        zt_hi = sb("zt_hi", [128, 2, KB, SE], F32R)
        zt_lo = sb("zt_lo", [128, 2, KB, SE], F32R)
        xt = sb("xt", [128, KB, 2 * T])
        xt_hi, xt_lo = sb("xt_hi", [128, KB, 2 * T], F32R), sb("xt_lo", [128, KB, 2 * T], F32R)
        q_hi, q_lo = sb("q_hi", [128, Q, 2 * T], F32R), sb("q_lo", [128, Q, 2 * T], F32R)
        k_hi, k_lo = sb("k_hi", [128, 2, S], F32R), sb("k_lo", [128, 2, S], F32R)
        kp = sb("kp", [128, HEADS, SE], F32R)
        qp = sb("qp", [128, HEADS, T], F32R)
        v = sb("v", [P, 2, C, D])
        z_first = v[:, 1, :, :]
        probs = sb("probs", [128, 2, PER_QUAD, S])
        probs_t = sb("probs_t", [P, PER_QUAD, C, T])
        row_max = sb("row_max", [T, 2, PER_QUAD])
        nbias = sb("nbias", [T, 2, PER_QUAD])
        row_sum = sb("row_sum", [T, 2, PER_QUAD])
        row_inv = sb("row_inv", [T, 2, PER_QUAD])
        ot_hi = sb("ot_hi", [128, 2, Q, T], F32R)
        ot_lo = sb("ot_lo", [128, 2, Q, T], F32R)
        rows = sb("rows", [T, D])
        mask_u8 = rows[0:B, :].bitcast(U8)[:, 0:PER_QUAD * S]

        ps_s = stack.enter_context(nc.psum_tensor("ps_s", [128, PER_QUAD, 512], F32))
        ps_t = stack.enter_context(nc.psum_tensor("ps_t", [128, 2, 512], F32))
        ps = stack.enter_context(nc.psum_tensor("ps", [128, 2, 512], F32))
        ps_o = ps_t[:, 0, C * T:C * T + T]

        ctx_loaded, xt_loaded, x_loaded = sem("ctx_loaded"), sem("xt_loaded"), sem("x_loaded")
        ctx0_loaded = [sem(f"ctx0_loaded{c}") for c in range(C)]
        ctx1_loaded = sem("ctx1_loaded")
        small_loaded, mask_loaded = sem("small_loaded"), sem("mask_loaded")
        raw_loaded = [sem(f"raw_loaded{i}") for i in range(2)]
        wq_loaded = sem("wq_loaded")
        mask_stored = sem("mask_stored")
        k_packed = [sem(f"k_packed{q}") for q in range(Q)]
        q_packed = [sem(f"q_packed{q}") for q in range(Q)]
        out_stored = sem("out_stored")
        z_done, k_done, v_done, q_done = sem("z_done"), sem("k_done"), sem("v_done"), sem("q_done")
        s_done, t_done = sem("s_done"), sem("t_done")
        o_done, y_done = sem("o_done"), sem("y_done")
        zf_ready, kh_ready, qh_ready, oh_ready = sem("zf_ready"), sem("kh_ready"), sem("qh_ready"), sem("oh_ready")
        v_ready, exp_ready, pt_ready, gate_ready = sem("v_ready"), sem("exp_ready"), sem("pt_ready"), sem("gate_ready")
        wh_ready, xh0_ready = sem("wh_ready"), sem("xh0_ready")
        zh_ready = sem("zh_ready")
        zl_ready, kl_ready, ql_ready, ol_ready = sem("zl_ready"), sem("kl_ready"), sem("ql_ready"), sem("ol_ready")
        y_ready, max_ready, nbias_ready = sem("y_ready"), sem("max_ready"), sem("nbias_ready")
        inv_ready, stats_ready, mv_ready, ln_stats = sem("inv_ready"), sem("stats_ready"), sem("mv_ready"), sem("ln_stats")
        wl_ready, mask_ready = sem("wl_ready"), sem("mask_ready")
        xl0_ready, wkh_dve = sem("xl0_ready"), sem("wkh_dve")
        ident_zero, ident_ready, consts_ready = sem("ident_zero"), sem("ident_ready"), sem("consts_ready")
        var_ready, rstd_ready, z_ready = sem("var_ready"), sem("rstd_ready"), sem("z_ready")
        p_ready, xh_ready, xl_ready = sem("p_ready"), sem("xh_ready"), sem("xl_ready")
        wkh_ready, wl_pool = sem("wkh_ready"), sem("wl_pool")

        def fixed(eng, value):
            return value if isinstance(value, int) else eng.to_reg(value)

        def odd_slot(j):
            return 2 * j + 1

        def even_slot(j):
            return 2 * j + 2

        block = stack.enter_context(nc.Block())

        @block.sync
        def _(sp):
            def load_ctx(b):
                sp.dma_start(z[:, :, :], ctx_in[b].rearrange("(p c) d -> p c d", c=C)).then_inc(ctx_loaded, DMA)

            def load_xt(p):
                sp.dma_start(xt[:, :, :], xT[p].rearrange("(k p) t -> p k t", p=128)).then_inc(xt_loaded, DMA)

            def load_weight(i, w, ks=slice(0, KB), loaded=None):
                sp.dma_start(raw[:, i, ks, :], w.rearrange("(k p) n -> p k n", p=128)[:, ks, :]).then_inc(
                    loaded or raw_loaded[i], DMA)

            def pack_q(q, par):
                for lines, src in ((0, q_hi), (1, q_hi), (2, q_lo)):
                    sp.dma_start(qp[lines * HD:(lines + 1) * HD, PER_QUAD * q:PER_QUAD * (q + 1), :].bitcast(F32),
                                 src[:, q, par * T:(par + 1) * T].bitcast(F32)).then_inc(q_packed[q], DMA)

            def pack_k(q, b):
                for lines, src in ((0, k_hi), (1, k_lo), (2, k_hi)):
                    sp.dma_start(kp[lines * HD:(lines + 1) * HD, PER_QUAD * q:PER_QUAD * (q + 1), 0:S].bitcast(F32),
                                 src[:, q % 2, :].bitcast(F32)).then_inc(k_packed[q], DMA)
                sp.dma_start(kp[3 * HD:3 * HD + 1, PER_QUAD * q:PER_QUAD * (q + 1), 0:S].bitcast(F32),
                             masks_dram[b].rearrange("(o g s) -> o g s", o=1, g=PER_QUAD)).then_inc(k_packed[q], DMA)

            def next_q(b, q, par_next, pair_next):
                count = fixed(sp, 2 * (4 * b + q + 1))
                sp.wait_ge(mask_stored, DMA)
                sp.wait_ge(s_done, count)
                count = fixed(sp, 4 * pair_next + q + 1)
                sp.wait_ge(mask_stored, DMA)
                sp.wait_ge(ql_ready, count)
                pack_q(q, par_next)

            def next_k(b, q):
                count = fixed(sp, 2 * (4 * (b - 1) + q + 1))
                sp.wait_ge(mask_stored, DMA)
                sp.wait_ge(s_done, count)
                count = fixed(sp, 4 * b + q + 1)
                sp.wait_ge(mask_stored, DMA)
                sp.wait_ge(kl_ready, count)
                pack_k(q, b)

            def slot(b, par_next, pair_next, first=False, last=False, xt_pair=None, load_ahead=True):
                if not first:
                    next_k(b, 3)
                else:
                    sp.wait_ge(kl_ready, 4)
                    pack_k(3, 0)
                if xt_pair is not None:
                    count = fixed(sp, xt_pair - 1)
                    sp.wait_ge(mask_stored, DMA)
                    sp.wait_ge(xl_ready, count)
                    load_xt(xt_pair)
                if not last:
                    next_q(b, 0, par_next, pair_next)
                if not first:
                    count = fixed(sp, b)
                    sp.wait_ge(mask_stored, DMA)
                    sp.wait_ge(y_ready, count)
                    sp.dma_start(out[b - 1], rows[:, :]).then_inc(out_stored, DMA)
                if not last:
                    next_q(b, 1, par_next, pair_next)
                    next_k(b + 1, 0)
                    next_q(b, 2, par_next, pair_next)
                if not first:
                    count = fixed(sp, DMA * b)
                    sp.wait_ge(mask_stored, DMA)
                    sp.wait_ge(out_stored, count)
                sp.dma_start(rows[:, :], x[b]).then_inc(x_loaded, DMA)
                if not last:
                    next_k(b + 1, 1)
                    next_q(b, 3, par_next, pair_next)
                    if load_ahead:
                        count = fixed(sp, 4 * (b + 3))
                        sp.wait_ge(mask_stored, DMA)
                        sp.wait_ge(z_done, count)
                        load_ctx(b + 3)
                    next_k(b + 1, 2)

            for c in range(C):
                sp.dma_start(z[:, c, :], ctx_in[0].rearrange("(p c) d -> p c d", c=C)[:, c, :]).then_inc(
                    ctx0_loaded[c], DMA)
            load_xt(0)
            load_weight(0, wqT, slice(0, KB // 2), wq_loaded)
            load_weight(0, wqT, slice(KB // 2, KB))
            for dst, src in ((gam, gamma), (bet, beta), (gate_sb, gate)):
                sp.dma_start(dst[:, :], src).then_inc(small_loaded, DMA)
            load_weight(1, wkT)
            sp.dma_start(mask_u8, mask4).then_inc(mask_loaded, DMA)
            sp.dma_start(z_first, ctx_in[1].rearrange("(p c) d -> p c d", c=C)).then_inc(ctx1_loaded, DMA)
            sp.wait_ge(wl_ready, KB)
            load_weight(0, wvT)
            sp.wait_ge(xl0_ready, 1)
            load_xt(1)
            sp.wait_ge(z_done, 4)
            load_ctx(2)
            sp.wait_ge(mask_ready, 1)
            sp.dma_start(masks_dram, probs[0:B, 0, :, :].rearrange("b g s -> b (g s)")).then_inc(mask_stored, DMA)
            sp.wait_ge(ql_ready, 1)
            pack_q(0, 0)
            sp.wait_ge(mask_stored, DMA)
            for q in range(3):
                sp.wait_ge(kl_ready, q + 1)
                pack_k(q, 0)
                sp.wait_ge(ql_ready, q + 2)
                pack_q(q + 1, 0)
                if q == 0:
                    sp.wait_ge(wl_pool, POOL_WK)
                    sp.wait_ge(wl_ready, 2 * KB - POOL_WK)
                    load_weight(1, woT)

            slot(0, 1, 0, first=True)
            with sp.Fori(0, LOOPS) as j:
                slot(odd_slot(j), 0, j + 1, xt_pair=j + 2)
                slot(even_slot(j), 1, j + 1)
            slot(B - 3, 0, LOOPS + 1, load_ahead=False)
            slot(B - 2, 1, LOOPS + 1, load_ahead=False)
            slot(B - 1, 0, 0, last=True)
            sp.wait_ge(y_ready, B)
            sp.dma_start(out[B - 1], rows[:, :]).then_inc(out_stored, DMA)
            sp.wait_ge(out_stored, DMA * B)

        @block.tensor
        def _(pe):
            def part3(dst, lhs, rhs, first, last):
                nc.tensor.matmul(dst, lhs[0], rhs[0], start=first, stop=False)
                nc.tensor.matmul(dst, lhs[0], rhs[1], start=False, stop=False)
                return nc.tensor.matmul(dst, lhs[1], rhs[0], start=False, stop=last)

            def project_k(q, par, bank, ks=range(KB)):
                for k in ks:
                    cols = slice(128 * q, 128 * (q + 1))
                    mm = part3(ps[:, bank, 0:SE], (wk_hi[:, k, cols], wk_lo[:, k, cols]),
                               (zt_hi[:, par, k, :], zt_lo[:, par, k, :]), k == 0, k == KB - 1)
                if ks[-1] == KB - 1:
                    mm.then_inc(k_done, 1)

            def project_v(c, par, bank, ks=range(KB)):
                for k in ks:
                    keys = slice(P * c, P * (c + 1))
                    mm = part3(ps[0:P, bank, 0:D], (zt_hi[:, par, k, keys], zt_lo[:, par, k, keys]),
                               (wv_hi[:, k, :], wv_lo[:, k, :]), k == 0, k == KB - 1)
                if ks[-1] == KB - 1:
                    mm.then_inc(v_done, 1)

            def project_q(q, dst, ks=range(KB)):
                for k in ks:
                    cols = slice(128 * q, 128 * (q + 1))
                    mm = part3(dst[:, 0:2 * T], (wq_hi[:, k, cols], wq_lo[:, k, cols]),
                               (xt_hi[:, k, :], xt_lo[:, k, :]), k == 0, k == KB - 1)
                if ks[-1] == KB - 1:
                    mm.then_inc(q_done, 1)

            def project_out(par, bank, ks=range(KB)):
                for k in ks:
                    mm = part3(ps[0:T, bank, 0:D], (ot_hi[:, par, k, :], ot_lo[:, par, k, :]),
                               (wo_hi[:, k, :], wo_lo[:, k, :]), k == 0, k == KB - 1)
                if ks[-1] == KB - 1:
                    mm.then_inc(y_done, 1)

            def transpose_z(k, dst, src=z):
                for c in range(C):
                    mm = nc.tensor.transpose(dst[:, P * c:P * (c + 1)], src[:, c, 128 * k:128 * (k + 1)],
                                             ident[0:P, 0:P])
                mm.then_inc(z_done, 1)

            def scores(b, q, first=False):
                pe.wait_ge(k_packed[q], 4 * DMA * (b + 1))
                pe.wait_ge(q_packed[q], 3 * DMA * (b + 1))
                for g in range(PER_QUAD):
                    if not first:
                        pe.wait_ge(exp_ready, 4 * (4 * b + q - 1) + g + 1)
                    h = PER_QUAD * q + g
                    mm = nc.tensor.matmul(ps_s[0:T, g, 0:SE], qp[0:PACKED, h, :], kp[0:PACKED, h, :],
                                          start=True, stop=True)
                    if g % 2:
                        mm.then_inc(s_done, 1)

            def transpose_p(n, par, g):
                for c in range(C):
                    mm = nc.tensor.transpose(ps_t[0:P, g % 2, T * c:T * (c + 1)],
                                             probs[0:T, par, g, P * c:P * (c + 1)], ident[0:T, 0:T])
                mm.then_inc(t_done, 1)

            def transpose_first(n, par, first=False):
                pe.wait_ge(p_ready, 4 * n + 1)
                if not first:
                    pe.wait_ge(pt_ready, 4 * n - 1)
                    pe.wait_ge(ol_ready, n)
                transpose_p(n, par, 0)
                pe.wait_ge(p_ready, 4 * n + 2)
                if not first:
                    pe.wait_ge(pt_ready, 4 * n)
                transpose_p(n, par, 1)

            def transpose_second(n, par):
                pe.wait_ge(p_ready, 4 * n + 3)
                pe.wait_ge(pt_ready, 4 * n + 1)
                transpose_p(n, par, 2)
                pe.wait_ge(p_ready, 4 * n + 4)
                pe.wait_ge(pt_ready, 4 * n + 2)
                transpose_p(n, par, 3)

            def times_v(b, q, par):
                n = 4 * b + q
                pe.wait_ge(pt_ready, 4 * n + 4)
                for c in range(C):
                    for g in range(PER_QUAD):
                        h = PER_QUAD * q + g
                        mm = nc.tensor.matmul(ps_o[HD * g:HD * (g + 1), :], v[:, par, c, HD * h:HD * (h + 1)],
                                              probs_t[:, g, c, :], start=(c == 0), stop=(c == C - 1))
                mm.then_inc(o_done, 1)

            def slot(b, par, first=False, last=False, with_z=True):
                with_q = par == 1 and not last
                with_z = with_z and not last
                k1_bank = 0 if with_z else 1
                n = 4 * b
                if first:
                    pe.wait_ge(kl_ready, 3)
                    project_v(1, 0, 0, [0, 1])
                    pe.wait_ge(zf_ready, 8)
                    pe.wait_ge(ql_ready, 4)
                scores(b, 0, first)
                if not first:
                    transpose_first(n - 1, 1)
                    pe.wait_ge(kl_ready, 4 * b + 3)
                    project_v(1, par, 0, [0])
                if not first:
                    transpose_second(n - 1, 1)
                project_v(1, par, 0, [2, 3] if first else [1, 2, 3])
                if not first:
                    times_v(b - 1, 3, 1 - par)
                pe.wait_ge(v_ready, 3 * b + 1)
                project_v(2, par, 1, [0, 1])
                project_v(2, par, 1, [2, 3])
                pe.wait_ge(v_ready, 3 * b + 2)
                if not last:
                    project_k(3, par, 0)
                scores(b, 1)
                transpose_first(n, 0, first)
                pe.wait_ge(v_ready, 3 * b + 3)
                if not first and not last:
                    pe.wait_ge(ol_ready, n)
                    project_out(1 - par, 1, [0])
                transpose_second(n, 0)
                if last:
                    project_k(3, par, 0)
                    pe.wait_ge(ol_ready, n)
                    project_out(1 - par, 1, [0])
                elif not first:
                    project_out(1 - par, 1, [1, 2, 3])
                if first:
                    times_v(b, 0, par)
                if with_z:
                    pe.wait_ge(z_ready, b + 3)
                    pe.wait_ge(kl_ready, 4 * b + 4)
                    transpose_z(0, ps[:, 0, :])
                if not first:
                    times_v(b, 0, par)
                if with_z:
                    if not first:
                        pe.wait_ge(y_ready, b)
                    transpose_z(1, ps[:, 1, :])
                if with_q:
                    pe.wait_ge(xl_ready, xt_count(b))
                    pe.wait_ge(zf_ready, 4 * (b + 2) + 1)
                    project_q(0, ps[:, 0, :])
                    pe.wait_ge(zf_ready, 4 * (b + 2) + 2)
                    project_q(1, ps[:, 1, :])
                scores(b, 2)
                transpose_first(n + 1, 1)
                if not last:
                    if with_q:
                        pe.wait_ge(ql_ready, q_count(b) + 1)
                    elif with_z:
                        pe.wait_ge(zf_ready, 4 * (b + 2) + 1)
                    else:
                        pe.wait_ge(kl_ready, 4 * b + 4)
                    pe.wait_ge(zl_ready, 4 * (b + 2))
                    project_k(0, 1 - par, 0, [0])
                transpose_second(n + 1, 1)
                if last:
                    project_out(1 - par, 1, [1, 2])
                else:
                    project_k(0, 1 - par, 0, [1, 2, 3])
                times_v(b, 1, par)
                if with_q:
                    pe.wait_ge(ql_ready, q_count(b) + 2)
                    project_q(2, ps[:, 1, :])
                elif with_z:
                    pe.wait_ge(zf_ready, 4 * (b + 2) + 2)
                    transpose_z(2, ps[:, 1, :])
                if not last:
                    if with_z:
                        pe.wait_ge(kl_ready, 4 * (b + 1) + 1)
                    else:
                        pe.wait_ge(y_ready, b)
                    project_k(1, 1 - par, k1_bank, [0])
                if not last:
                    project_k(1, 1 - par, k1_bank, [1, 2, 3])
                scores(b, 3)
                transpose_first(n + 2, 0)
                if with_q:
                    if with_z:
                        pe.wait_ge(ql_ready, q_count(b) + 3)
                        transpose_z(2, ps[:, 1, :])
                elif with_z:
                    pe.wait_ge(zf_ready, 4 * (b + 2) + 3)
                    transpose_z(3, ps[:, 1, :])
                transpose_second(n + 2, 0)
                if with_q:
                    pe.wait_ge(kl_ready, 4 * (b + 1) + 2)
                    project_q(3, ps[:, 0, :])
                    times_v(b, 2, par)
                    if with_z:
                        pe.wait_ge(zf_ready, 4 * (b + 2) + 3)
                        transpose_z(3, ps[:, 1, :])
                    pe.wait_ge(ql_ready, q_count(b) + 4)
                    project_k(2, 1 - par, 0, [0])
                    project_k(2, 1 - par, 0, [1, 2, 3])
                    pe.wait_ge(zf_ready, 4 * (b + 2) + 4)
                    project_v(0, 1 - par, 1)
                elif not last:
                    if with_z:
                        pe.wait_ge(kl_ready, 4 * (b + 1) + 2)
                    else:
                        pe.wait_ge(kl_ready, 4 * (b + 1) + 1)
                    project_k(2, 1 - par, 0)
                    times_v(b, 2, par)
                    if with_z:
                        pe.wait_ge(zf_ready, 4 * (b + 2) + 4)
                    else:
                        pe.wait_ge(kl_ready, 4 * (b + 1) + 2)
                    project_v(0, 1 - par, 1, [0])
                    project_v(0, 1 - par, 1, [1, 2, 3])
                else:
                    project_out(1 - par, 1, [3])
                    times_v(b, 2, par)

            def q_count(b):
                return 2 * (b + 1)

            pe.wait_ge(ident_ready, 1)
            for _ in range(WARM_UP):
                nc.tensor.transpose(ps_t[:, 0, 0:128], ident[:, :], ident[:, :])
            pe.wait_ge(xl0_ready, 1)
            for k in range(KB // 2):
                pe.wait_ge(wl_ready, k + 1)
                project_q(0, ps[:, 0, :], [k])
            pe.wait_ge(z_ready, 1)
            for k in range(KB):
                transpose_z(k, ps_s[:, k, :])
            for k in range(KB // 2, KB):
                pe.wait_ge(wl_ready, k + 1)
                project_q(0, ps[:, 0, :], [k])
            project_q(1, ps[:, 1, :])
            project_q(2, ps_t[:, 0, :])
            project_q(3, ps_t[:, 1, :])
            pe.wait_ge(consts_ready, 4)
            pe.wait_ge(ql_ready, 1)
            for k in range(KB):
                pe.wait_ge(zl_ready, k + 1)
                if k < POOL_WK:
                    pe.wait_ge(wl_pool, k + 1)
                else:
                    pe.wait_ge(wl_ready, KB + k - POOL_WK + 1)
                project_k(0, 0, 0, [k])
            pe.wait_ge(ql_ready, 2)
            project_k(1, 0, 1)
            pe.wait_ge(kl_ready, 1)
            project_k(2, 0, 0)
            pe.wait_ge(kl_ready, 2)
            for k in range(KB):
                if k == 2:
                    pe.wait_ge(z_ready, 2)
                    for block in range(KB):
                        pe.wait_ge(zf_ready, block + 1)
                        transpose_z(block, ps_s[:, block, :], z_first)
                if k < POOL_WV:
                    pe.wait_ge(wl_pool, POOL_WK + k + 1)
                else:
                    pe.wait_ge(wl_ready, 2 * KB - POOL_WK + k - POOL_WV + 1)
                project_v(0, 0, 1, [k])
            slot(0, 0, first=True)
            pe.wait_ge(wl_pool, POOL_WK + POOL_WV + KB)
            with pe.Fori(0, LOOPS) as j:
                xt_count = lambda b: j + 1
                slot(odd_slot(j), 1)
                slot(even_slot(j), 0)
            xt_count = lambda b: (b - 1) // 2 + 1
            slot(B - 3, 1)
            slot(B - 2, 0, with_z=False)
            slot(B - 1, 1, last=True)
            n = 4 * B - 1
            pe.wait_ge(kl_ready, 4 * B)
            pe.wait_ge(ol_ready, n - 1)
            project_out(1, 0, [0, 1])
            pe.wait_ge(ol_ready, n)
            project_out(1, 0, [2])
            transpose_first(n, 1)
            transpose_second(n, 1)
            times_v(B - 1, 3, 1)
            pe.wait_ge(ol_ready, n + 1)
            project_out(1, 0, [3])

        @block.scalar
        def _(act):
            def high(dst, src, done, count, ready):
                act.wait_ge(done, count)
                nc.scalar.activation(dst, src, ACT.Copy).then_inc(ready, 1)

            def affine_z(b, k, src, first=False):
                if not first:
                    act.wait_ge(zl_ready, 4 * b + k - 1)
                act.wait_ge(z_done, 4 * b + k + 1)
                nc.scalar.activation(zt_full[:, k % 2, :], src[:, 0:S], ACT.Identity, bias=bet[:, k:k + 1],
                                     scale=gam[:, k:k + 1]).then_inc(zf_ready, 1)

            def high_k(b, q, bank, before):
                if before is not None:
                    act.wait_ge(k_packed[before[1]], 4 * DMA * (before[0] + 1))
                high(k_hi[:, q % 2, :], ps[:, bank, 0:S], k_done, 4 * b + q + 1, kh_ready)

            def high_q(base, q, src):
                high(q_hi[:, q, :], src[:, 0:2 * T], q_done, base + q + 1, qh_ready)

            def next_q(b, q, bank):
                act.wait_ge(q_packed[q], 3 * DMA * (b + 1))
                high_q(2 * (b + 1), q, ps[:, bank, :])

            def high_o(n, par, q):
                high(ot_hi[:, par, q, :], ps_o, o_done, n + 1, oh_ready)

            def copy_v(b, par, c, bank):
                act.wait_ge(v_done, 3 * b + c + 1)
                nc.scalar.activation(v[:, par, c, :], ps[0:P, bank, 0:D], ACT.Copy).then_inc(v_ready, 1)

            def exps(n, par, heads):
                for g in heads:
                    if g % 2 == 0:
                        act.wait_ge(nbias_ready, 2 * n + g // 2 + 1)
                    nc.scalar.activation(probs[0:T, par, g, :], ps_s[0:T, g, 0:S], ACT.Exp,
                                         bias=nbias[:, par, g:g + 1], scale=SCALE,
                                         accum_out=row_sum[:, par, g:g + 1]).then_inc(exp_ready, 1)

            def copy_pt(n, heads):
                for g in heads:
                    act.wait_ge(t_done, 4 * n + g + 1)
                    nc.scalar.activation(probs_t[:, g, :, :].rearrange("p c t -> p (c t)"),
                                         ps_t[0:P, g % 2, 0:C * T], ACT.Copy).then_inc(pt_ready, 1)

            def split_high(w_hi, i, count, first_half=None):
                if first_half is not None:
                    act.wait_ge(first_half, DMA)
                for k in range(KB):
                    if k == (0 if first_half is None else KB // 2):
                        act.wait_ge(raw_loaded[i], DMA * count)
                    nc.scalar.activation(w_hi[:, k, :], raw[:, i, k, :], ACT.Copy).then_inc(wh_ready, 1)

            def slot(b, par, first=False, last=False, with_z=True):
                n = 4 * b
                with_q = par == 1 and not last
                with_z = with_z and not last
                if not first:
                    copy_v(b, par, 0, 1)
                    copy_pt(n - 1, [0, 1, 2, 3])
                exps(n, 0, [0, 1, 2])
                copy_v(b, par, 1, 0)
                exps(n, 0, [3])
                if not first:
                    high_o(n - 1, 1 - par, 3)
                copy_v(b, par, 2, 1)
                if first:
                    split_high(wo_hi, 1, 2)
                if not last:
                    high_k(b, 3, 0, (b, 1))
                copy_pt(n, [0, 1])
                copy_pt(n, [2, 3])
                exps(n + 1, 1, [0, 1])
                if last:
                    high_k(b, 3, 0, (b, 1))
                exps(n + 1, 1, [2, 3])
                if not with_q:
                    high_o(n, par, 0)
                if with_z:
                    affine_z(b + 2, 0, ps[:, 0, :])
                if with_q:
                    high_o(n, par, 0)
                if with_z:
                    affine_z(b + 2, 1, ps[:, 1, :])
                if with_q:
                    next_q(b, 0, 0)
                    next_q(b, 1, 1)
                copy_pt(n + 1, [0, 1])
                copy_pt(n + 1, [2, 3])
                exps(n + 2, 0, [0])
                if not last:
                    high_k(b + 1, 0, 0, (b, 2))
                exps(n + 2, 0, [1, 2])
                if with_z and not with_q:
                    affine_z(b + 2, 2, ps[:, 1, :])
                exps(n + 2, 0, [3])
                if with_q:
                    next_q(b, 2, 1)
                high_o(n + 1, par, 1)
                if not last:
                    high_k(b + 1, 1, 0 if with_z else 1, (b, 3))
                copy_pt(n + 2, [0, 1])
                if with_z:
                    affine_z(b + 2, 2 if with_q else 3, ps[:, 1, :])
                copy_pt(n + 2, [2, 3])
                exps(n + 3, 1, [0])
                if with_q:
                    next_q(b, 3, 0)
                    exps(n + 3, 1, [1, 2])
                    high_o(n + 2, par, 2)
                    exps(n + 3, 1, [3])
                    affine_z(b + 2, 3, ps[:, 1, :])
                    high_k(b + 1, 2, 0, (b + 1, 0))
                else:
                    exps(n + 3, 1, [1])
                    if not last:
                        high_k(b + 1, 2, 0, (b + 1, 0))
                    exps(n + 3, 1, [2, 3])
                    high_o(n + 2, par, 2)

            act.wait_ge(xt_loaded, DMA)
            nc.scalar.activation(xt_hi[:, :, :], xt[:, :, :], ACT.Copy).then_inc(xh0_ready, 1)

            split_high(wq_hi, 0, 1, first_half=wq_loaded)
            act.wait_ge(small_loaded, 3 * DMA)
            for k in range(KB):
                affine_z(0, k, ps_s[:, k, :], first=(k < 2))
            high_q(0, 0, ps[:, 0, :])
            high_q(0, 1, ps[:, 1, :])
            high_q(0, 2, ps_t[:, 0, :])
            act.wait_ge(mask_loaded, DMA)
            nc.scalar.activation(probs[0:B, 0, :, :].rearrange("b g s -> b (g s)"), mask_u8, ACT.Copy, bias=-MASKED,
                                 scale=MASKED).then_inc(mask_ready, 1)
            high_q(0, 3, ps_t[:, 1, :])
            nc.scalar.activation(gate_t[:, :], gate_sb[:, :], ACT.Tanh).then_inc(gate_ready, 1)
            split_high(wv_hi, 0, 2)
            high_k(0, 0, 0, None)
            high_k(0, 1, 1, None)
            for k in range(2):
                affine_z(1, k, ps_s[:, k, :])
            high_k(0, 2, 0, (0, 0))
            for k in range(2, KB):
                affine_z(1, k, ps_s[:, k, :])
            copy_v(0, 0, 0, 1)
            slot(0, 0, first=True)
            with act.Fori(0, LOOPS) as j:
                slot(odd_slot(j), 1)
                slot(even_slot(j), 0)
            slot(B - 3, 1)
            slot(B - 2, 0, with_z=False)
            slot(B - 1, 1, last=True)
            n = 4 * B - 1
            copy_pt(n, [0, 1, 2, 3])
            high_o(n, 1, 3)

        @block.vector
        def _(dve):
            def low(dst, hi, src, high_ready, count, ready):
                dve.wait_ge(high_ready, count)
                nc.vector.tensor_tensor(dst, src, hi.bitcast(F32), ALU.subtract).then_inc(ready, 1)

            def split_z(b, par, k):
                dve.wait_ge(zf_ready, 4 * b + k + 1)
                nc.vector.tensor_copy(zt_hi[:, par, k, 0:S], zt_full[:, k % 2, :]).then_inc(zh_ready, 1)
                low(zt_lo[:, par, k, 0:S], zt_hi[:, par, k, 0:S], zt_full[:, k % 2, :], zh_ready, 4 * b + k + 1,
                    zl_ready)

            def low_k(b, q, bank):
                low(k_lo[:, q % 2, :], k_hi[:, q % 2, :], ps[:, bank, 0:S], kh_ready, 4 * b + q + 1, kl_ready)

            def low_q(base, q, src):
                low(q_lo[:, q, :], q_hi[:, q, :], src[:, 0:2 * T], qh_ready, base + q + 1, ql_ready)

            def low_o(n, par, q):
                low(ot_lo[:, par, q, :], ot_hi[:, par, q, :], ps_o, oh_ready, n + 1, ol_ready)

            def maxima(n, par):
                for half in range(2):
                    heads = slice(2 * half, 2 * half + 2)
                    dve.wait_ge(s_done, 2 * n + half + 1)
                    nc.vector.tensor_reduce(row_max[:, par, heads], ps_s[0:T, heads, 0:S], AX.X,
                                            ALU.max).then_inc(max_ready, 1)
                    dve.wait_ge(max_ready, 2 * n + half + 1)
                    nc.vector.tensor_scalar(nbias[:, par, heads], row_max[:, par, heads], LEAST_MAX, -SCALE, ALU.max,
                                            ALU.mult).then_inc(nbias_ready, 1)

            def inverses(n, par, half):
                heads = slice(2 * half, 2 * half + 2)
                dve.wait_ge(exp_ready, 4 * n + 2 * half + 2)
                nc.vector.reciprocal(row_inv[:, par, heads], row_sum[:, par, heads]).then_inc(inv_ready, 1)

            def normalise_probs(n, par, half):
                dve.wait_ge(inv_ready, 2 * n + half + 1)
                for g in (2 * half, 2 * half + 1):
                    nc.vector.tensor_scalar(probs[0:T, par, g, :], probs[0:T, par, g, :], row_inv[:, par, g:g + 1],
                                            1.0, ALU.mult, ALU.mult).then_inc(p_ready, 1)

            def ln_statistics(b, src=z):
                for c in range(C):
                    if isinstance(b, int) and b == 0:
                        dve.wait_ge(ctx0_loaded[c], DMA)
                    nc.vector.bn_stats(stats[:, c, :], src[:, c, :]).then_inc(stats_ready, 1)
                count = fixed(dve, C * (b + 1))
                dve.wait_ge(stats_ready, C)
                dve.wait_ge(stats_ready, count)
                for c in range(C):
                    nc.vector.bn_aggr(mv[:, c, :], stats[:, c, :]).then_inc(mv_ready, 1)
                dve.wait_ge(mv_ready, C * (b + 1))
                nc.vector.tensor_scalar(neg_mean[:, :], mv[:, :, 0], -1.0, None, ALU.mult).then_inc(ln_stats, 1)
                nc.vector.tensor_scalar(var_eps[:, :], mv[:, :, 1], EPS, None, ALU.add).then_inc(ln_stats, 1)

            def residual(b, bank):
                dve.wait_ge(y_done, b + 1)
                dve.wait_ge(x_loaded, DMA * (b + 1))
                nc.vector.scalar_tensor_tensor(rows[:, :], ps[0:T, bank, 0:D], gate_t[0:T, 0:1], rows[:, :], ALU.mult,
                                               ALU.add).then_inc(y_ready, 1)

            def slot(b, par, first=False, last=False, with_z=True):
                n = 4 * b
                with_q = par == 1 and not last
                with_z = with_z and not last
                base = 2 * (b + 1)
                maxima(n, 0)
                if first:
                    inverses(n, 0, 0)
                    inverses(n, 0, 1)
                if with_z:
                    if first:
                        dve.wait_ge(z_ready, 2)
                    dve.wait_ge(ctx_loaded, DMA * (b + 1))
                    ln_statistics(b + 2)
                if not first:
                    inverses(n, 0, 0)
                    low_o(n - 1, 1 - par, 3)
                    inverses(n, 0, 1)
                if not last:
                    low_k(b, 3, 0)
                maxima(n + 1, 1)
                if last:
                    low_k(b, 3, 0)
                inverses(n + 1, 1, 0)
                if not first and not last:
                    residual(b - 1, 1)
                inverses(n + 1, 1, 1)
                if not with_q:
                    low_o(n, par, 0)
                if with_z:
                    split_z(b + 2, par, 0)
                if with_q:
                    low_o(n, par, 0)
                if with_z:
                    split_z(b + 2, par, 1)
                if with_q:
                    low_q(base, 0, ps[:, 0, :])
                    low_q(base, 1, ps[:, 1, :])
                maxima(n + 2, 0)
                if not last:
                    low_k(b + 1, 0, 0)
                inverses(n + 2, 0, 0)
                low_o(n + 1, par, 1)
                inverses(n + 2, 0, 1)
                if with_q:
                    low_q(base, 2, ps[:, 1, :])
                elif with_z:
                    split_z(b + 2, par, 2)
                if not last:
                    low_k(b + 1, 1, 0 if with_z else 1)
                maxima(n + 3, 1)
                if with_z:
                    split_z(b + 2, par, 2 if with_q else 3)
                if with_q:
                    low_q(base, 3, ps[:, 0, :])
                elif not last:
                    low_k(b + 1, 2, 0)
                if last:
                    dve.wait_ge(p_ready, 4 * (n + 3))
                inverses(n + 3, 1, 0)
                if last:
                    normalise_probs(n + 3, 1, 0)
                low_o(n + 2, par, 2)
                inverses(n + 3, 1, 1)
                if last:
                    normalise_probs(n + 3, 1, 1)
                if with_q:
                    split_z(b + 2, par, 3)
                    low_k(b + 1, 2, 0)
                if last:
                    residual(b - 1, 1)

            def split_low(w_hi, w_lo, i, high_count, ks=range(KB)):
                for k in ks:
                    low(w_lo[:, k, :], w_hi[:, k, :], raw[:, i, k, :], wh_ready, high_count + k + 1, wl_ready)

            ln_statistics(0)
            low(xt_lo[:, :, :], xt_hi[:, :, :], xt[:, :, :], xh0_ready, 1, xl0_ready)
            split_low(wq_hi, wq_lo, 0, 0)
            for k in range(KB):
                split_z(0, 0, k)
            low_q(0, 0, ps[:, 0, :])
            dve.wait_ge(raw_loaded[1], DMA)
            for k in range(POOL_WK, KB):
                nc.vector.tensor_copy(wk_hi[:, k, :], raw[:, 1, k, :]).then_inc(wkh_dve, 1)
                low(wk_lo[:, k, :], wk_hi[:, k, :], raw[:, 1, k, :], wkh_dve, k - POOL_WK + 1, wl_ready)
            low_q(0, 1, ps[:, 1, :])
            dve.wait_ge(z_ready, 1)
            dve.wait_ge(ctx1_loaded, DMA)
            ln_statistics(1, z_first)
            low_k(0, 0, 0)
            low_q(0, 2, ps_t[:, 0, :])
            low_q(0, 3, ps_t[:, 1, :])
            split_low(wv_hi, wv_lo, 0, KB, range(POOL_WV, KB))
            low_k(0, 1, 1)
            split_z(1, 1, 0)
            low_k(0, 2, 0)
            for k in range(1, KB):
                split_z(1, 1, k)
            dve.wait_ge(gate_ready, 1)
            slot(0, 0, first=True)
            with dve.Fori(0, LOOPS) as j:
                slot(odd_slot(j), 1)
                slot(even_slot(j), 0)
            slot(B - 3, 1)
            slot(B - 2, 0, with_z=False)
            slot(B - 1, 1, last=True)
            n = 4 * B - 1
            low_o(n, 1, 3)
            residual(B - 1, 0)

        @block.gpsimd
        def _(pool):
            def normalise(b, src=z):
                pool.wait_ge(ln_stats, 2 * (b + 1))
                nc.gpsimd.tensor_tensor(rstd[:, :], var_eps[:, :], minus_half[:, :], ALU.pow).then_inc(rstd_ready, 1)
                count = fixed(pool, b + 1)
                pool.wait_ge(consts_ready, 4)
                pool.wait_ge(rstd_ready, count)
                for c in range(C):
                    last = nc.gpsimd.tensor_scalar(src[:, c, :], src[:, c, :], neg_mean[:, c:c + 1], rstd[:, c:c + 1],
                                                   ALU.add, ALU.mult)
                last.then_inc(z_ready, 1)

            def split_xt(pair):
                pool.wait_ge(xt_loaded, DMA * (pair + 1))
                count = fixed(pool, 4 * pair)
                pool.wait_ge(consts_ready, 4)
                pool.wait_ge(q_done, count)
                nc.gpsimd.tensor_scalar(xt_hi[:, :, :], xt[:, :, :], 1.0, 1.0, ALU.mult, ALU.mult).then_inc(xh_ready, 1)
                pool.wait_ge(xh_ready, pair)
                nc.gpsimd.tensor_tensor(xt_lo[:, :, :], xt[:, :, :], xt_hi[:, :, :].bitcast(F32),
                                        ALU.subtract).then_inc(xl_ready, 1)

            def normalise_probs(n, par):
                for g in range(PER_QUAD):
                    if g % 2 == 0:
                        count = fixed(pool, 2 * n + g // 2 + 1)
                        pool.wait_ge(consts_ready, 4)
                        pool.wait_ge(inv_ready, count)
                    nc.gpsimd.tensor_scalar(probs[0:T, par, g, :], probs[0:T, par, g, :], row_inv[:, par, g:g + 1],
                                            1.0, ALU.mult, ALU.mult).then_inc(p_ready, 1)

            def split_low(w_hi, w_lo, i, high_count, ks):
                for k in ks:
                    pool.wait_ge(wh_ready, high_count + k + 1)
                    nc.gpsimd.tensor_tensor(w_lo[:, k, :], raw[:, i, k, :], w_hi[:, k, :].bitcast(F32),
                                            ALU.subtract).then_inc(wl_pool, 1)

            def slot(b, xt_pair=None, with_z=True, first=False, last=False):
                normalise_probs(4 * b, 0)
                if with_z:
                    normalise(b + 2)
                for q in range(1, Q - 1 if last else Q):
                    normalise_probs(4 * b + q, q % 2)
                    if first and q == 2:
                        split_low(wo_hi, wo_lo, 1, 2 * KB, range(KB))
                if xt_pair is not None:
                    split_xt(xt_pair)

            nc.gpsimd.memset(minus_half[:, :], -0.5).then_inc(consts_ready, 1)
            pool.wait_ge(consts_ready, 1)
            nc.gpsimd.memset(qp[3 * HD:3 * HD + 1, :, :].bitcast(F32), 1.0).then_inc(consts_ready, 1)
            pool.wait_ge(consts_ready, 2)
            nc.gpsimd.memset(ident[:, :], 0.0).then_inc(ident_zero, 1)
            pool.wait_ge(ident_zero, 1)
            nc.gpsimd.affine_select(out=ident[:, :], in_=ident[:, :], compare_op=ALU.not_equal, fill=1.0, base=0,
                                    pattern=[[-1, 128]], channel_multiplier=1).then_inc(ident_ready, 1)
            nc.gpsimd.memset(zt_hi[:, :, :, S:SE].bitcast(F32), 0.0)
            nc.gpsimd.memset(zt_lo[:, :, :, S:SE].bitcast(F32), 0.0).then_inc(consts_ready, 1)
            nc.gpsimd.memset(kp[:, :, S:SE].bitcast(F32), 0.0).then_inc(consts_ready, 1)
            pool.wait_ge(ident_ready, 1)
            pool.wait_ge(consts_ready, 4)
            normalise(0)

            pool.wait_ge(raw_loaded[1], DMA)
            for k in range(POOL_WK):
                nc.gpsimd.tensor_scalar(wk_hi[:, k, :], raw[:, 1, k, :], 1.0, 1.0, ALU.mult,
                                        ALU.mult).then_inc(wkh_ready, 1)
                pool.wait_ge(wkh_ready, k + 1)
                nc.gpsimd.tensor_tensor(wk_lo[:, k, :], raw[:, 1, k, :], wk_hi[:, k, :].bitcast(F32),
                                        ALU.subtract).then_inc(wl_pool, 1)
            split_low(wv_hi, wv_lo, 0, KB, range(POOL_WV))
            normalise(1, z_first)
            slot(0, 1, first=True)
            with pool.Fori(0, LOOPS) as j:
                slot(odd_slot(j))
                slot(even_slot(j), j + 2)
            slot(B - 3)
            slot(B - 2, with_z=False)
            slot(B - 1, with_z=False, last=True)


def kernel(x, ctx_2048, mask_BxS2_bf1, L0_xattn_Wq, L0_xattn_Wk, L0_xattn_Wv, L0_xattn_Wo, L0_xattn_ln_gamma,
           L0_xattn_ln_beta, L0_xattn_gate):
    import numpy as np
    import concourse.bacc as bacc
    from concourse.bass_utils import run_bass_kernel_spmd

    B, T, D = x.shape
    S = ctx_2048.shape[1]
    C, HD, KB = 3, D // HEADS, D // 128

    def heads_inner(w):
        return w.T.reshape(D, D // 128, PER_QUAD, HD).transpose(0, 1, 3, 2).reshape(D, D)

    mask = np.asarray(mask_BxS2_bf1).view(np.uint8).reshape(B, 1, S // C, C).transpose(0, 1, 3, 2)
    arrays = {
        "x": x,
        "xT": np.asarray(x).reshape(B // 2, 2 * T, D).transpose(0, 2, 1),
        "ctx_in": ctx_2048,
        "mask4": np.broadcast_to(mask, (B, PER_QUAD, C, S // C)).reshape(B, PER_QUAD * S),
        "wqT": heads_inner(np.asarray(L0_xattn_Wq)),
        "wkT": heads_inner(np.asarray(L0_xattn_Wk)),
        "wvT": np.asarray(L0_xattn_Wv).T,
        "woT": np.asarray(L0_xattn_Wo).T,
        "gamma": np.asarray(L0_xattn_ln_gamma).reshape(KB, 128).T,
        "beta": np.asarray(L0_xattn_ln_beta).reshape(KB, 128).T,
        "gate": np.broadcast_to(np.asarray(L0_xattn_gate), (128, 1)),
    }
    arrays = {k: np.ascontiguousarray(a) for k, a in arrays.items()}
    nc = bacc.Bacc("TRN2", target_bir_lowering=False, num_devices=1)
    aps = {k: nc.dram_tensor(k, a.shape, mybir.dt.from_np(a.dtype), kind="ExternalInput").ap()
           for k, a in arrays.items()}
    masks_dram = nc.dram_tensor("masks_dram", (B, PER_QUAD * S), F32, kind="Internal").ap()
    out = nc.dram_tensor("out", (B, T, D), F32, kind="ExternalOutput").ap()
    build(nc, **aps, masks_dram=masks_dram, out=out)
    r = run_bass_kernel_spmd(nc, [arrays], core_ids=[0])
    return r.results[0]["out"]
```
